# Optimizing a Trainium2 kernel written in Bass

```python
import numpy as np
import jax
import jax.numpy as jnp

def _softmax(x, axis=-1):
    return jax.nn.softmax(x, axis=axis)

def _gelu(x):
    return jax.nn.gelu(x, approximate=True)

def _silu(x):
    return jax.nn.silu(x)

def _sigmoid(x):
    return jax.nn.sigmoid(x)

def _layernorm(x, axis=-1, eps=1e-05):
    m = jnp.mean(x, axis=axis, keepdims=True)
    v = jnp.var(x, axis=axis, keepdims=True)
    return (x - m) / jnp.sqrt(v + eps)

def _scatter_add(tgt, idx, src, axis=0):
    return tgt.at[idx].add(src)

def _segment_sum(src, seg, n):
    return jax.ops.segment_sum(src, seg, n)
kernel_name = 'mk_seq_postln_d1_jaxref_r8_bc7341'

def setup_inputs(seed: int=0):
    np.random.seed(seed)
    _w = jnp.asarray

    def _L0_attn_setup():
        import math
        import jax, jax.numpy as jnp
        import numpy as np
        B, T, C, H, DQK, DV = (2, 256, 128, 16, 64, 64)
        key = jax.random.key(seed)
        ks = jax.random.split(key, 5)
        x = jax.random.normal(ks[0], (B, T, C), dtype=jnp.float32)
        w_q = jax.random.normal(ks[1], (H, DQK, C), dtype=jnp.float32) / math.sqrt(C)
        w_k = jax.random.normal(ks[2], (H, DQK, C), dtype=jnp.float32) / math.sqrt(C)
        w_v = jax.random.normal(ks[3], (H, DV, C), dtype=jnp.float32) / math.sqrt(C)
        w_o = jax.random.normal(ks[4], (DV * H, C), dtype=jnp.float32) / math.sqrt(C)
        return {'x': x, 'w_q': w_q, 'w_k': w_k, 'w_v': w_v, 'w_o': w_o}
    _L0_attn_in = _L0_attn_setup()

    def _L0_ffn_setup():
        import jax, jax.numpy as jnp
        import numpy as np
        H = 128
        I = 128
        E = 8
        key = jax.random.key(seed)
        ks = jax.random.split(key, 8)
        s = 0.02
        x = jax.random.normal(ks[0], (4, 256, H), dtype=jnp.float32)
        Wg = jax.random.normal(ks[1], (H, E), dtype=jnp.float32) * s
        bg = jnp.zeros((E,), dtype=jnp.float32)
        W1 = jax.random.normal(ks[2], (E, H, I), dtype=jnp.float32) * s
        b1 = jnp.zeros((E, I), dtype=jnp.float32)
        W2 = jax.random.normal(ks[3], (E, I, H), dtype=jnp.float32) * s
        b2 = jnp.zeros((E, H), dtype=jnp.float32)
        return {'x': x, 'Wg': Wg, 'bg': bg, 'W1': W1, 'b1': b1, 'W2': W2, 'b2': b2}
    _L0_ffn_in = _L0_ffn_setup()
    _d = {'L0_attn_x': _L0_attn_in['x'], 'L0_attn_w_q': _L0_attn_in['w_q'], 'L0_attn_w_k': _L0_attn_in['w_k'], 'L0_attn_w_v': _L0_attn_in['w_v'], 'L0_attn_w_o': _L0_attn_in['w_o'], 'L0_ffn_Wg': _L0_ffn_in['Wg'], 'L0_ffn_bg': _L0_ffn_in['bg'], 'L0_ffn_W1': _L0_ffn_in['W1'], 'L0_ffn_b1': _L0_ffn_in['b1'], 'L0_ffn_W2': _L0_ffn_in['W2'], 'L0_ffn_b2': _L0_ffn_in['b2']}
    _x0 = _d['L0_attn_x']
    _d['L0_attn_x'] = jax.random.normal(jax.random.fold_in(jax.random.key(seed), 1), (8, 512, 128), dtype=_x0.dtype)
    del _x0
    return _d

def reference(L0_attn_x, L0_attn_w_q, L0_attn_w_k, L0_attn_w_v, L0_attn_w_o, L0_ffn_Wg, L0_ffn_bg, L0_ffn_W1, L0_ffn_b1, L0_ffn_W2, L0_ffn_b2):

    def _L0_attn_ref(x, w_q, w_k, w_v, w_o):
        import math
        import jax, jax.numpy as jnp
        import numpy as np
        B, T, C, H, DQK, DV = (2, 256, 128, 16, 64, 64)
        n, t, c = x.shape
        q = jnp.einsum('ntc,hdc->nhtd', x, w_q)
        k = jnp.einsum('ntc,hdc->nhtd', x, w_k)
        v = jnp.einsum('ntc,hdc->nhtd', x, w_v)
        scale = 1.0 / math.sqrt(w_q.shape[1])
        a = jnp.einsum('nhtd,nhsd->nhts', q, k) * scale
        causal = jnp.arange(t)[:, None] < jnp.arange(t)[None, :]
        a = jnp.where(causal[None, None, :, :], -jnp.inf, a)
        a = jax.nn.softmax(a, axis=3)
        y = jnp.einsum('nhts,nhsd->nthd', a, v).reshape(n, t, -1)
        return y @ w_o

    def _L0_ffn_ref(x, Wg, bg, W1, b1, W2, b2):
        import jax, jax.numpy as jnp
        import numpy as np
        H = 128
        I = 128
        E = 8
        B, S, Hd = x.shape
        xf = x.reshape(-1, Hd)
        logits = xf @ Wg + bg
        gates = jax.nn.softmax(logits, axis=-1)
        idx = jnp.argmax(gates, axis=-1)
        h = jax.nn.gelu(jnp.einsum('th,ehi->tei', xf, W1) + b1, approximate=False)
        y = jnp.einsum('tei,eih->teh', h, W2) + b2
        out = jnp.take_along_axis(y, idx[:, None, None], axis=1)[:, 0, :]
        return out.reshape(B, S, Hd)
    x = L0_attn_x
    x = _layernorm(x + _L0_attn_ref(x, L0_attn_w_q, L0_attn_w_k, L0_attn_w_v, L0_attn_w_o), axis=-1)
    x = _layernorm(x + _L0_ffn_ref(x, L0_ffn_Wg, L0_ffn_bg, L0_ffn_W1, L0_ffn_b1, L0_ffn_W2, L0_ffn_b2), axis=-1)
    return x

_drawn_inputs = setup_inputs


def setup_inputs(seed=0):
    import zlib

    import numpy as np

    out = dict(_drawn_inputs(seed))
    spreads = {'L0_ffn_bg': (0.0, 0.1), 'L0_ffn_b1': (0.0, 0.701), 'L0_ffn_b2': (0.0, 0.1)}
    factors = {}
    for name, (base, spread) in spreads.items():
        noise = np.random.default_rng([zlib.crc32(name.encode()), seed]).standard_normal(out[name].shape)
        drawn = base * np.exp(spread * noise) if base else spread * noise
        out[name] = jnp.asarray(drawn.astype(out[name].dtype))
    for name, factor in factors.items():
        out[name] = (out[name] * factor).astype(out[name].dtype)
    return out
```

```python
from contextlib import ExitStack

import concourse.bass as bass
from concourse import mybir

F32 = mybir.dt.float32
F32R = mybir.dt.float32r
BF16 = mybir.dt.bfloat16
ACT = mybir.ActivationFunctionType
ALU = mybir.AluOpType
AX = mybir.AxisListType

P = 128
MASKED = -1e30
LN_EPS = 1e-5


def layer(nc, x, xT, wq, wk, wv, wo, Wg, bg, W1, W2, b12, out):
    B, C, S = xT.shape
    PAIRS = wq.shape[0]
    E = Wg.shape[1]
    D = P // 2
    NT = S // P
    TILES = B * NT
    STEPS = B * PAIRS
    QSCALE = float(D) ** -0.5
    assert C == P and NT == 4

    with ExitStack() as ctx:
        def sb(name, shape, dt):
            return ctx.enter_context(nc.sbuf_tensor(name, shape, dt))

        def sem(name):
            return ctx.enter_context(nc.semaphore(name))

        x_sb = sb("x_sb", [P, TILES, C], F32)
        meanvar = sb("meanvar", [P, TILES, 2], F32)
        rstd1 = sb("rstd1", [P, TILES], F32)
        ident = sb("ident", [P, P], F32)
        zeros = sb("zeros", [P, E * P], F32)
        carrier = sb("carrier", [P, 5], F32)
        eps = sb("eps", [P, TILES], F32)
        minus_half = sb("minus_half", [P, TILES], F32)
        stats = sb("stats", [P, NT, 6], F32)
        aggr = sb("aggr", [P, NT, 2], F32)
        w1_hi = sb("w1_hi", [P, E, P], F32R)
        w1_lo = sb("w1_lo", [P, E, P], F32R)
        w2_hi = sb("w2_hi", [P, E, P], F32R)
        w2_lo = sb("w2_lo", [P, E, P], F32R)
        w1_raw = sb("w1_raw", [P, E, P], F32)
        w2_raw = sb("w2_raw", [P, E, P], F32)
        wg_raw = sb("wg_raw", [P, E], F32)
        wg_halves = sb("wg_halves", [P, 2, E], F32R)
        bg_sb = sb("bg_sb", [P, E], F32)
        b_raw = sb("b_raw", [E, 2 * P], F32)
        b_halves = sb("b_halves", [E, 2, 2 * P], F32R)
        rank = sb("rank", [P, E], F32)
        pick_raw = sb("pick_raw", [E, E, P], F32)
        pick = sb("pick", [E, E, P], F32R)

        attn = ctx.enter_context(ExitStack())

        def sb1(name, shape, dt):
            return attn.enter_context(nc.sbuf_tensor(name, shape, dt))

        xT_32 = sb1("xT_32", [P, B, S], F32)
        xT_hi = sb1("xT_hi", [P, B, S], F32R)
        xT_lo = sb1("xT_lo", [P, B, S], F32R)
        xT_now = sb1("xT_now", [P, 2, S], F32R)
        wqk_halves = sb1("wqk_halves", [P, PAIRS, 2, 2, C], F32R)
        wqk_now = sb1("wqk_now", [P, 2, 2, C], F32R)
        wvo_hi = sb1("wvo_hi", [P, PAIRS, 2 * C], F32R)
        wvo_lo = sb1("wvo_lo", [P, PAIRS, 2 * C], F32R)
        ident_bf = sb1("ident_bf", [P, P], BF16)
        mask_bf = sb1("mask_bf", [P, P], BF16)
        g_32 = sb1("g_32", [P, 2, S], F32)
        g_hi = sb1("g_hi", [P, 2, S], F32R)
        g_lo = sb1("g_lo", [P, 2, S], F32R)
        u_sb = sb1("u_sb", [P, NT, 2 * C], F32)
        negmax = sb1("negmax", [P, NT, 2], F32)
        sums = sb1("sums", [P, NT, 2], F32)
        rsums = sb1("rsums", [P, NT, 2], F32)
        with ExitStack() as setup:
            def sb0(name, shape, dt):
                return setup.enter_context(nc.sbuf_tensor(name, shape, dt))

            wq_sb = sb0("wq_sb", [P, PAIRS, C], F32)
            wk_sb = sb0("wk_sb", [P, PAIRS, C], F32)
            wqk_raw = sb0("wqk_raw", [P, PAIRS, 2, C], F32)
            wv_sb = sb0("wv_sb", [P, PAIRS, C], F32)
            wo_sb = sb0("wo_sb", [P, PAIRS, C], F32)
            wvo_raw = sb0("wvo_raw", [P, PAIRS, 2 * C], F32)
        probs = sb1("probs", [P, 2, 2, S], F32)
        pT = sb1("pT", [P, 6, S], F32)

        attn.close()
        x1_now = sb("x1_now", [P, NT, C], F32)
        x1T_hi = sb("x1T_hi", [P, S], F32R)
        x1T_lo = sb("x1T_lo", [P, S], F32R)
        logits = sb("logits", [P, NT, E], F32)
        best = sb("best", [P, NT], F32)
        ranked = sb("ranked", [P, NT, E], F32)
        first = sb("first", [P, NT], F32)
        chosen = sb("chosen", [P, NT, E], F32)
        chosenT = sb("chosenT", [E, B, S], F32R)
        spread = sb("spread", [P, 2, E, S], BF16)
        m1_hi = sb("m1_hi", [P, E, S], F32R)
        m1_lo = sb("m1_lo", [P, E, S], F32R)
        h_32 = sb("h_32", [P, S], F32)
        h_hi = sb("h_hi", [P, S], F32R)
        h_lo = sb("h_lo", [P, S], F32R)
        m2_hi = sb("m2_hi", [P, E, S], F32R)
        m2_lo = sb("m2_lo", [P, E, S], F32R)
        yT_sb = sb("yT_sb", [P, S], F32)
        r2 = sb("r2", [P, NT, C], F32)
        rstd2 = sb("rstd2", [P, NT], F32)
        out_sb = sb("out_sb", [P, NT, C], F32)

        bank = [ctx.enter_context(nc.psum_tensor(f"bank{i}", [P, S], F32)) for i in range(8)]
        s_bank = [[bank[0], bank[1]], [bank[2], bank[3]]]
        t_bank = [bank[4], bank[5]]
        y_bank = [bank[6], bank[7]]

        x1T_bank, logits_bank, h_bank, yT_bank, back_bank, chosenT_bank = (bank[n] for n in (0, 1, 4, 5, 6, 7))
        spread_bank = [bank[2], bank[3]]

        def live(g):
            return not isinstance(g, int) or 0 <= g < B

        def first(g):
            return isinstance(g, int) and g == 0

        def expert_slots(engine, slots):
            for g in range(-2, 2):
                slots(g, g % 2)
            with engine.Fori(1, B // 2 - 1) as half:
                for parity in range(2):
                    slots(half * 2 + parity, parity)
            for g in range(B - 2, B + 2):
                slots(g, g % 2)

        x_loaded = sem("x_loaded")
        wq_loaded = sem("wq_loaded")
        wk_loaded = sem("wk_loaded")
        wv_loaded = sem("wv_loaded")
        wo_loaded = sem("wo_loaded")
        xT_loaded = sem("xT_loaded")
        wqk_moved = sem("wqk_moved")
        pool_zero = sem("pool_zero")
        consts_ready = sem("consts_ready")
        xT_split = sem("xT_split")
        xT_moved = sem("xT_moved")
        wqk_psum = sem("wqk_psum")
        wqk_copied = sem("wqk_copied")
        wqk_split = sem("wqk_split")
        wvo_split = sem("wvo_split")
        half_xT = sem("half_xT")
        half_wqk = sem("half_wqk")
        half_wvo = sem("half_wvo")
        g_psum = sem("g_psum")
        u_psum = sem("u_psum")
        g_rounded = sem("g_rounded")
        u_copied_act = sem("u_copied_act")
        u_copied_dve = sem("u_copied_dve")
        wvo_psum = sem("wvo_psum")
        wvo_copied = sem("wvo_copied")
        g_split = sem("g_split")
        g_joined = sem("g_joined")
        scores_ready = sem("scores_ready")
        negmax_ready = sem("negmax_ready")
        probs_ready = sem("probs_ready")
        tr_psum = sem("tr_psum")
        tr_dve = sem("tr_dve")
        tr_act = sem("tr_act")
        y_psum = sem("y_psum")
        rsums_ready = sem("rsums_ready")
        y_added = sem("y_added")
        stats_ready = sem("stats_ready")
        aggr_ready = sem("aggr_ready")
        meanvar_ready = sem("meanvar_ready")
        w_loaded = sem("w_loaded")
        bg_loaded = sem("bg_loaded")
        b_loaded = sem("b_loaded")
        w_rounded = sem("w_rounded")
        w_split = sem("w_split")
        small_raw = sem("small_raw")
        small_rounded = sem("small_rounded")
        small_split = sem("small_split")
        var1_ready = sem("var1_ready")
        var2_ready = sem("var2_ready")
        rstd1_ready = sem("rstd1_ready")
        x1_ready = sem("x1_ready")
        x1_kept = sem("x1_kept")
        x1T_psum = sem("x1T_psum")
        x1T_rounded = sem("x1T_rounded")
        x1T_split = sem("x1T_split")
        logits_psum = sem("logits_psum")
        logits_ready = sem("logits_ready")
        argmax_step = sem("argmax_step")
        chosen_ready = sem("chosen_ready")
        chosenT_psum = sem("chosenT_psum")
        chosenT_ready = sem("chosenT_ready")
        spread_psum = sem("spread_psum")
        spread_ready = sem("spread_ready")
        m1_dve = sem("m1_dve")
        m1_pool = sem("m1_pool")
        h_psum = sem("h_psum")
        h_ready = sem("h_ready")
        h_rounded = sem("h_rounded")
        h_split = sem("h_split")
        m2_dve = sem("m2_dve")
        m2_pool = sem("m2_pool")
        yT_psum = sem("yT_psum")
        yT_copied = sem("yT_copied")
        back_psum = sem("back_psum")
        r2_ready = sem("r2_ready")
        r2_stats = sem("r2_stats")
        r2_aggr = sem("r2_aggr")
        rstd2_ready = sem("rstd2_ready")
        out_ready = sem("out_ready")
        stored = sem("stored")

        block = ctx.enter_context(nc.Block())

        @block.sync
        def _(sp):
            sp.dma_start(wq_sb[:, :, :], wq.rearrange("a p c -> p a c")).then_inc(wq_loaded, 16)
            sp.dma_start(wk_sb[:, :, :], wk.rearrange("a p c -> p a c")).then_inc(wk_loaded, 16)
            sp.dma_start(xT_32[:, :, :], xT.rearrange("b c s -> c b s")).then_inc(xT_loaded, 16)
            sp.dma_start(wv_sb[:, :, :], wv.rearrange("a p c -> p a c")).then_inc(wv_loaded, 16)
            sp.dma_start(wo_sb[:, :, :], wo.rearrange("a p c -> p a c")).then_inc(wo_loaded, 16)
            sp.dma_start(x_sb[:, :, :], x.rearrange("(t p) c -> p t c", p=P)).then_inc(x_loaded, 16)
            sp.dma_start(w1_raw[:, :, :], W1).then_inc(w_loaded, 16)
            sp.dma_start(w2_raw[:, :, :], W2).then_inc(w_loaded, 16)
            sp.dma_start(wg_raw[:, :], Wg).then_inc(w_loaded, 16)
            sp.dma_start(bg_sb[:, :], bg.broadcast_to([P, E])).then_inc(bg_loaded, 16)
            sp.dma_start(b_raw[:, :], b12).then_inc(w_loaded, 16)

            def move_wqk(pair):
                sp.dma_start(wqk_now[:, :, :, :].rearrange("p a h c -> p (a h c)").bitcast(F32),
                             wqk_halves[:, bass.ds(pair, 1), :, :, :].rearrange("p n a h c -> p (n a h c)").bitcast(F32)
                             ).then_inc(wqk_moved, 16)

            def next_wqk(n, pair):
                sp.wait_ge(g_psum, 2 * n)
                move_wqk(pair)

            def move_xT(b):
                for half, src in enumerate((xT_hi, xT_lo)):
                    sp.dma_start(xT_now[:, half, :].bitcast(F32),
                                 src[:, bass.ds(b, 1), :].rearrange("p n s -> p (n s)").bitcast(F32)
                                 ).then_inc(xT_moved, 16)

            sp.wait_ge(wqk_split, 1)
            move_wqk(0)
            sp.wait_ge(xT_split, B)
            move_xT(0)
            with sp.Fori(0, B - 1) as b:
                with sp.Fori(0, PAIRS - 1) as p:
                    next_wqk(b * PAIRS + p + 1, p + 1)
                next_wqk(b * PAIRS + PAIRS, 0)
                sp.wait_ge(u_psum, b * PAIRS + PAIRS)
                move_xT(b + 1)
            with sp.Fori(0, PAIRS - 1) as p:
                next_wqk((B - 1) * PAIRS + p + 1, p + 1)
            next_wqk(B * PAIRS, 0)

            def keep_x1(g):
                sp.wait_ge(x1_ready, g + 1)
                sp.dma_start(x_sb[:, bass.ds(g * NT, NT), :], x1_now[:, :, :]).then_inc(x1_kept, 16)

            def store(g):
                sp.wait_ge(out_ready, g + 1)
                sp.dma_start(out_groups[bass.ds(g, 1)].rearrange("n p t c -> (n p) t c"), out_sb[:, :, :]
                             ).then_inc(stored, 16)

            out_groups = out.rearrange("(g t p) c -> g p t c", p=P, t=NT)
            for g in range(4):
                keep_x1(g)
            with sp.Fori(4, B) as g:
                keep_x1(g)
                store(g - 4)
            for g in range(B - 4, B):
                store(g)
            sp.wait_ge(stored, 16 * B)

        @block.gpsimd
        def _(pool):
            pool.memset(ident[:, :], 0.0).then_inc(pool_zero, 1)
            pool.memset(ident_bf[:, :], 0.0).then_inc(pool_zero, 1)
            pool.memset(mask_bf[:, :], 0.0).then_inc(pool_zero, 1)
            pool.memset(zeros[:, :], 0.0).then_inc(pool_zero, 1)
            pool.wait_ge(pool_zero, 4)
            for t in (ident, ident_bf):
                pool.affine_select(out=t[:, :], in_=t[:, :], compare_op=ALU.not_equal, fill=1.0, base=0,
                                   pattern=[[-1, P]], channel_multiplier=1).then_inc(consts_ready, 1)
            pool.affine_select(out=mask_bf[:, :], in_=mask_bf[:, :], compare_op=ALU.is_ge, fill=MASKED, base=0,
                               pattern=[[-1, P]], channel_multiplier=1).then_inc(consts_ready, 1)

            pool.wait_ge(xT_loaded, 16)
            for b in range(B):
                pool.tensor_tensor(xT_hi[:, b, :], xT_32[:, b, :], zeros[:, 0:S], ALU.add).then_inc(half_xT, 1)
            for b in range(B):
                pool.wait_ge(half_xT, b + 1)
                pool.tensor_tensor(xT_lo[:, b, :], xT_32[:, b, :], xT_hi[:, b, :].bitcast(F32), ALU.subtract
                                   ).then_inc(xT_split, 1)

            def join_g(n):
                pool.wait_ge(g_split, 2 * n + 2)
                pool.tensor_tensor(g_32[:, :, :], g_hi[:, :, :].bitcast(F32), g_lo[:, :, :].bitcast(F32), ALU.add
                                   ).then_inc(g_joined, 1)

            join_g(0)
            for e in range(E):
                pool.memset(rank[:, e:e + 1], float(E - e)).then_inc(small_raw, 1)
            pool.memset(pick_raw[:, :, :], 0.0).then_inc(small_raw, 1)
            pool.memset(eps[:, :], LN_EPS).then_inc(small_raw, 1)
            pool.memset(minus_half[:, :], -0.5).then_inc(small_raw, 1)
            pool.wait_ge(small_raw, E + 3)
            pool.affine_select(out=pick_raw[:, :, :], in_=pick_raw[:, :, :], compare_op=ALU.not_equal, fill=1.0,
                               base=0, pattern=[[-1, E], [0, P]], channel_multiplier=1).then_inc(small_raw, 1)
            pool.wait_ge(small_raw, E + 4)
            pool.tensor_tensor(pick[:, :, :].rearrange("k e p -> k (e p)"),
                               pick_raw[:, :, :].rearrange("k e p -> k (e p)"), zeros[0:E, :], ALU.add).then_inc(small_rounded, 1)
            pool.wait_ge(w_loaded, 64)
            flat = [t[:, :, :].rearrange("p e i -> p (e i)") for t in (w1_raw, w1_hi, w1_lo, w2_raw, w2_hi, w2_lo)]
            parts = (flat[0:3], flat[3:6], (wg_raw[:, :], wg_halves[:, 0, :], wg_halves[:, 1, :]),
                     (b_raw[:, :], b_halves[:, 0, :], b_halves[:, 1, :]))
            for raw, hi, lo in parts:
                pool.tensor_tensor(hi, raw, zeros[0:raw.shape[0], 0:raw.shape[1]], ALU.add).then_inc(w_rounded, 1)
            pool.wait_ge(w_rounded, 4)
            for raw, hi, lo in parts:
                pool.tensor_tensor(lo, raw, hi.bitcast(F32), ALU.subtract).then_inc(w_split, 1)

            def joins(b):
                with pool.Fori(0, PAIRS) as p:
                    join_g(b * PAIRS + p + 1)

            def first_rstd(tiles, batches):
                pool.wait_ge(meanvar_ready, batches)
                n = tiles.stop - tiles.start
                pool.tensor_tensor(rstd1[:, tiles], meanvar[:, tiles, 1], eps[:, 0:n], ALU.add).then_inc(var1_ready, 1)
                pool.wait_ge(var1_ready, batches - B + 2)
                pool.tensor_tensor(rstd1[:, tiles], rstd1[:, tiles], minus_half[:, 0:n], ALU.pow
                                   ).then_inc(rstd1_ready, 1)

            with pool.Fori(0, B - 1) as b:
                joins(b)
            first_rstd(slice(0, TILES - NT), B - 1)
            joins(B - 1)
            first_rstd(slice(TILES - NT, TILES), B)

            def slots(g, parity):
                if live(g - 1):
                    pool.wait_ge(h_split, g)
                    if not first(g - 1):
                        pool.wait_ge(yT_psum, g - 1)
                    for e in range(E):
                        pool.tensor_tensor(m2_lo[:, e, :], h_lo[:, :].bitcast(F32), spread[:, 1 - parity, e, :], ALU.mult
                                           ).then_inc(m2_pool, 1)
                if live(g - 2):
                    pool.wait_ge(r2_aggr, g - 1)
                    pool.tensor_tensor(rstd2[:, :], aggr[:, :, 1], eps[:, 0:NT], ALU.add).then_inc(var2_ready, 1)
                    pool.wait_ge(var2_ready, g - 1)
                    pool.tensor_tensor(rstd2[:, :], rstd2[:, :], minus_half[:, 0:NT], ALU.pow
                                       ).then_inc(rstd2_ready, 1)
                if live(g + 1):
                    pool.wait_ge(x1T_split, g + 2)
                    if not first(g + 1):
                        pool.wait_ge(h_psum, g + 1)
                    for e in range(E):
                        pool.wait_ge(spread_ready, (g + 1) * E + e + 1)
                        pool.tensor_tensor(m1_lo[:, e, :], x1T_lo[:, :].bitcast(F32), spread[:, 1 - parity, e, :],
                                           ALU.mult).then_inc(m1_pool, 1)

            expert_slots(pool, slots)

        @block.tensor
        def _(pe):
            def three(out_ap, a_hi, a_lo, b_hi, b_lo, **last):
                pe.matmul(out_ap, a_lo, b_hi, start=True, stop=False)
                pe.matmul(out_ap, a_hi, b_lo, start=False, stop=False)
                return pe.matmul(out_ap, a_hi, b_hi, start=False, stop=True)

            def batch_of(t, b, w=slice(0, S)):
                return t[:, bass.ds(b, 1), w].rearrange("p n s -> p (n s)")

            def project_g(n, b):
                pe.wait_ge(wqk_moved, 16 * (n + 1))
                for h in range(2):
                    three(s_bank[0][h][:, :], wqk_now[:, 0, h, :], wqk_now[:, 1, h, :], batch_of(xT_hi, b),
                          batch_of(xT_lo, b)).then_inc(g_psum, 1)

            def project_u(pair, b):
                pe.wait_ge(xT_moved, 32 * b + 32)
                for j in range(NT):
                    t = slice(j * P, (j + 1) * P)
                    c = slice(j % 2 * 2 * C, (j % 2 + 1) * 2 * C)
                    last = three(y_bank[j // 2][:, c], xT_now[:, 0, t], xT_now[:, 1, t], wvo_hi[:, pair, :],
                                 wvo_lo[:, pair, :])
                last.then_inc(u_psum, 1)

            def scores(slot, i, b):
                w = (i + 1) * P
                t = slice(i * P, w)
                parts = ((g_lo, xT_hi), (g_hi, xT_lo), (g_hi, xT_hi)) if i else ((g_32, xT_32),)
                for h in range(2):
                    for n, (a, c) in enumerate(parts):
                        pe.matmul(s_bank[slot][h][:, 0:w], a[:, h, t], batch_of(c, b, slice(0, w)), start=(n == 0), stop=False)
                    pe.matmul(s_bank[slot][h][:, t], ident_bf[:, :], mask_bf[:, :], start=False, stop=True
                              ).then_inc(scores_ready, 1)

            def transposes(use, slot, blocks):
                for n, (h, j) in enumerate(blocks):
                    last = pe.transpose(t_bank[use % 2][:, n * P:(n + 1) * P], probs[:, slot, h, j * P:(j + 1) * P],
                                        ident[:, :])
                last.then_inc(tr_psum, 1)

            def pu(use, i, h, first=0):
                at = ((3 - i) % 2 * 2 + h) * C
                for j in range(i + 1):
                    last = pe.matmul(y_bank[(3 - i) // 2][:, at:at + C],
                                     pT[:, use, (first + j) * P:(first + j + 1) * P],
                                     u_sb[:, j, h * C:(h + 1) * C], start=(j == 0), stop=(j == i))
                last.then_inc(y_psum, 1)

            def step(g, p, b, b_next):
                pe.wait_ge(g_split, 2 * (g + 1))
                scores(0, 3, b)
                scores(1, 2, b)
                pe.wait_ge(y_added, 8 * g + 1)
                project_u(p, b)
                pe.wait_ge(probs_ready, 8 * g + 1)
                transposes(0, 0, [(0, j) for j in range(4)])
                pe.wait_ge(probs_ready, 8 * g + 2)
                transposes(1, 0, [(1, j) for j in range(4)])
                scores(0, 1, b)
                pe.wait_ge(u_copied_act, g + 1)
                pe.wait_ge(u_copied_dve, g + 1)
                pe.wait_ge(tr_dve, 2 * g + 1)
                pu(0, 3, 0)
                pe.wait_ge(tr_act, 4 * g + 1)
                pu(1, 3, 1)
                pe.wait_ge(probs_ready, 8 * g + 3)
                transposes(2, 1, [(0, j) for j in range(3)])
                pe.wait_ge(probs_ready, 8 * g + 4)
                transposes(3, 1, [(1, j) for j in range(3)])
                pe.wait_ge(g_joined, g + 1)
                scores(1, 0, b)
                pe.wait_ge(tr_dve, 2 * g + 2)
                pu(2, 2, 0)
                pe.wait_ge(tr_act, 4 * g + 2)
                pu(3, 2, 1)
                pe.wait_ge(probs_ready, 8 * g + 6)
                project_g(g + 1, b_next)
                transposes(4, 0, [(h, j) for h in range(2) for j in range(2)])
                pe.wait_ge(probs_ready, 8 * g + 8)
                transposes(5, 1, [(0, 0), (1, 0)])
                pe.wait_ge(tr_act, 4 * g + 3)
                pu(4, 1, 0)
                pu(4, 1, 1, first=2)
                pe.wait_ge(tr_act, 4 * g + 4)
                pu(5, 0, 0)
                pu(5, 0, 1, first=1)

            def weight_products(a, c, banks, done):
                for n in range(2 * PAIRS):
                    r = slice(n % 2 * D, (n % 2 + 1) * D)
                    m = n // 2 % 4
                    last = pe.matmul(banks[n % 2 * 2 + n // 8][:, m * C:(m + 1) * C], a[r, n // 2, :], c[r, n // 2, :],
                                     start=True, stop=True)
                last.then_inc(done, 1)

            pe.wait_ge(wq_loaded, 16)
            pe.wait_ge(wk_loaded, 16)
            weight_products(wq_sb, wk_sb, bank[0:4], wqk_psum)
            pe.wait_ge(wv_loaded, 16)
            pe.wait_ge(wo_loaded, 16)
            weight_products(wv_sb, wo_sb, bank[4:8], wvo_psum)
            pe.wait_ge(wqk_split, 1)
            pe.wait_ge(xT_split, B)
            project_g(0, 0)
            pe.wait_ge(consts_ready, 3)
            pe.wait_ge(wvo_split, 1)
            with pe.Fori(0, B - 1) as b:
                with pe.Fori(0, PAIRS - 1) as p:
                    step(b * PAIRS + p, p, b, b)
                step(b * PAIRS + PAIRS - 1, PAIRS - 1, b, b + 1)
            with pe.Fori(0, PAIRS) as p:
                step((B - 1) * PAIRS + p, p, B - 1, B - 1)

            def slots(g, parity):
                def first_layer(experts):
                    for e in experts:
                        pe.wait_ge(m1_dve, g * E + e + 1)
                        pe.wait_ge(m1_pool, g * E + e + 1)
                        for w, m in ((w1_hi, m1_lo), (w1_lo, m1_hi), (w1_hi, m1_hi)):
                            pe.matmul(h_bank[:, :], w[:, e, :], m[:, e, :], start=(e == 0 and w is w1_hi and m is m1_lo),
                                      stop=False)

                def bias(out_bank, half_of, k, done):
                    for n in (1, 0):
                        last = pe.matmul(out_bank[:, :], b_halves[:, n, half_of],
                                         chosenT[:, bass.ds(k, 1), :].rearrange("e n s -> e (n s)"), start=False,
                                         stop=(n == 0))
                    last.then_inc(done, 1)

                if live(g + 1):
                    pe.wait_ge(x1_ready, g + 2)
                    for i in range(NT):
                        last = pe.transpose(x1T_bank[:, i * P:(i + 1) * P], x1_now[:, i, :], ident[:, :])
                    last.then_inc(x1T_psum, 1)
                if live(g):
                    if not first(g):
                        pe.wait_ge(h_ready, g)
                    first_layer(range(0, 3))
                if live(g + 1):
                    pe.wait_ge(x1T_split, g + 2)
                    for i in range(NT):
                        t = slice(i * P, (i + 1) * P)
                        last = three(logits_bank[:, i * E:(i + 1) * E], x1T_hi[:, t], x1T_lo[:, t], wg_halves[:, 0, :],
                                     wg_halves[:, 1, :])
                    last.then_inc(logits_psum, 1)
                if live(g):
                    first_layer(range(3, 6))
                if live(g - 2):
                    pe.wait_ge(yT_copied, g - 1)
                    for i in range(NT):
                        t = slice(i * P, (i + 1) * P)
                        last = pe.transpose(back_bank[:, t], yT_sb[:, t], ident[:, :])
                    last.then_inc(back_psum, 1)
                if live(g):
                    first_layer(range(6, E))
                    bias(h_bank, slice(0, P), g, h_psum)
                if live(g + 1):
                    pe.wait_ge(chosen_ready, g + 2)
                    for i in range(NT):
                        last = pe.transpose(chosenT_bank[0:E, i * P:(i + 1) * P], chosen[:, i, :], ident[:, :])
                    last.then_inc(chosenT_psum, 1)
                for e in range(E):
                    if live(g + 1):
                        if e == 0:
                            pe.wait_ge(chosenT_ready, g + 2)
                        if e >= 2 or not first(g + 1):
                            pe.wait_ge(spread_ready, (g + 1) * E + e - 1)
                    if live(g - 1):
                        pe.wait_ge(m2_dve, (g - 1) * E + e + 1)
                        pe.wait_ge(m2_pool, (g - 1) * E + e + 1)
                        for w, m in ((w2_hi, m2_lo), (w2_lo, m2_hi), (w2_hi, m2_hi)):
                            pe.matmul(yT_bank[:, :], w[:, e, :], m[:, e, :], start=(e == 0 and w is w2_hi and m is m2_lo),
                                      stop=False)
                    if live(g + 1):
                        pe.matmul(spread_bank[e % 2][:, :], pick[:, e, :],
                                  chosenT[:, bass.ds(g + 1, 1), :].rearrange("e n s -> e (n s)"), start=True, stop=True
                                  ).then_inc(spread_psum, 1)
                if live(g - 1):
                    bias(yT_bank, slice(P, 2 * P), g - 1, yT_psum)

            pe.wait_ge(w_split, 4)
            pe.wait_ge(small_rounded, 1)
            expert_slots(pe, slots)

        @block.scalar
        def _(act):
            def round_g(n):
                for h in range(2):
                    act.wait_ge(g_psum, 2 * n + h + 1)
                    act.activation(g_hi[:, h, :], s_bank[0][h][:, :], ACT.Copy).then_inc(g_rounded, 1)

            def copy_u(n):
                act.wait_ge(u_psum, n + 1)
                act.activation(u_sb[:, 0:2, :].rearrange("p a c -> p (a c)"), y_bank[0][:, :], ACT.Copy
                               ).then_inc(u_copied_act, 1)

            def exps(g, slot, i, h, wait):
                w = (i + 1) * P
                if wait:
                    act.wait_ge(negmax_ready, 5 * g + wait)
                act.activation(probs[:, slot, h, 0:w], s_bank[slot][h][:, 0:w], ACT.Exp,
                               bias=negmax[:, i, h:h + 1], accum_out=sums[:, i, h:h + 1]).then_inc(probs_ready, 1)

            def copy_tr(g, count, bank_no, dst, w):
                act.wait_ge(tr_psum, 6 * g + count)
                act.activation(dst, t_bank[bank_no][:, w], ACT.Copy).then_inc(tr_act, 1)

            round_g(0)
            with act.Fori(0, STEPS) as g:
                exps(g, 0, 3, 0, 1)
                exps(g, 0, 3, 1, 2)
                exps(g, 1, 2, 0, 3)
                copy_u(g)
                copy_tr(g, 2, 1, pT[:, 1, :], slice(0, S))
                exps(g, 1, 2, 1, 0)
                exps(g, 0, 1, 0, 4)
                exps(g, 0, 1, 1, 0)
                copy_tr(g, 4, 1, pT[:, 3, 0:3 * P], slice(0, 3 * P))
                exps(g, 1, 0, 0, 5)
                exps(g, 1, 0, 1, 0)
                round_g(g + 1)
                copy_tr(g, 5, 0, pT[:, 4, :], slice(0, S))
                copy_tr(g, 6, 1, pT[:, 5, 0:2 * P], slice(0, 2 * P))

            def slots(g, parity):
                if live(g - 2):
                    act.wait_ge(yT_psum, g - 1)
                    if not first(g - 2):
                        act.wait_ge(back_psum, g - 2)
                    act.activation(yT_sb[:, :], yT_bank[:, :], ACT.Copy).then_inc(yT_copied, 1)
                if live(g + 1):
                    act.wait_ge(x1T_psum, g + 2)
                    if not first(g + 1):
                        act.wait_ge(m1_dve, (g + 1) * E)
                    act.activation(x1T_hi[:, :], x1T_bank[:, :], ACT.Copy).then_inc(x1T_rounded, 1)
                if live(g):
                    act.wait_ge(h_psum, g + 1)
                    if not first(g):
                        act.wait_ge(m2_dve, g * E)
                    act.activation(h_32[:, :], h_bank[:, :], ACT.Gelu).then_inc(h_ready, 1)
                    act.wait_ge(h_ready, g + 1)
                    act.activation(h_hi[:, :], h_32[:, :], ACT.Copy).then_inc(h_rounded, 1)
                if live(g + 1):
                    if live(g - 1):
                        act.wait_ge(m2_dve, g * E)
                        act.wait_ge(m2_pool, g * E)
                    for e in range(E):
                        act.wait_ge(spread_psum, (g + 1) * E + e + 1)
                        act.activation(spread[:, 1 - parity, e, :], spread_bank[e % 2][:, :], ACT.Copy
                                       ).then_inc(spread_ready, 1)

            expert_slots(act, slots)

        @block.vector
        def _(dve):
            def split_g(n):
                for h in range(2):
                    dve.wait_ge(g_rounded, 2 * n + h + 1)
                    dve.tensor_tensor(g_lo[:, h, :], s_bank[0][h][:, :], g_hi[:, h, :].bitcast(F32), ALU.subtract
                                      ).then_inc(g_split, 1)

            def copy_u(n):
                dve.wait_ge(u_psum, n + 1)
                dve.tensor_copy(u_sb[:, 2:4, :].rearrange("p a c -> p (a c)"), y_bank[1][:, :]
                                ).then_inc(u_copied_dve, 1)

            def copy_tr(g, count, bank_no, dst, w):
                dve.wait_ge(tr_psum, 6 * g + count)
                dve.tensor_copy(dst, t_bank[bank_no][:, w]).then_inc(tr_dve, 1)

            def wait_for(signal, count, cell):
                dve.wait_ge(signal, count)
                dve.memset(carrier[:, cell:cell + 1], 0.0)

            dve.wait_ge(wqk_psum, 1)
            for n in range(4):
                h, m = n // 2, n % 2 * 4
                dve.tensor_scalar(wqk_raw[:, m:m + 4, h, :], bank[n][:, :].rearrange("p (a c) -> p a c", c=C),
                                  QSCALE, None, ALU.mult).then_inc(wqk_copied, 1)
            dve.wait_ge(wqk_copied, 4)
            dve.tensor_copy(wqk_halves[:, :, 0, :, :], wqk_raw[:, :, :, :]).then_inc(half_wqk, 1)
            dve.wait_ge(half_wqk, 1)
            dve.tensor_tensor(wqk_halves[:, :, 1, :, :], wqk_raw[:, :, :, :], wqk_halves[:, :, 0, :, :].bitcast(F32),
                              ALU.subtract).then_inc(wqk_split, 1)
            dve.wait_ge(wvo_psum, 1)
            for n in range(4):
                h, m = n // 2, n % 2 * 4
                dve.tensor_copy(wvo_raw[:, m:m + 4, h * C:(h + 1) * C],
                                bank[4 + n][:, :].rearrange("p (a c) -> p a c", c=C)).then_inc(wvo_copied, 1)
            dve.wait_ge(wvo_copied, 4)
            dve.tensor_copy(wvo_hi[:, :, :], wvo_raw[:, :, :]).then_inc(half_wvo, 1)
            dve.wait_ge(half_wvo, 1)
            dve.tensor_tensor(wvo_lo[:, :, :], wvo_raw[:, :, :], wvo_hi[:, :, :].bitcast(F32),
                              ALU.subtract).then_inc(wvo_split, 1)
            split_g(0)
            dve.memset(carrier[:, :], 0.0).then_inc(y_added, 1)
            dve.wait_ge(x_loaded, 16)

            def neg_max(g, n, slot, i):
                w = (i + 1) * P
                for h in range(2):
                    dve.wait_ge(scores_ready, 8 * g + 2 * n + h + 1)
                    last = dve.tensor_reduce(negmax[:, i, h:h + 1], s_bank[slot][h][:, 0:w], AX.X, ALU.max,
                                             negate=True)
                    if n == 0 or h == 1:
                        last.then_inc(negmax_ready, 1)

            def add_y(g, n, tile0):
                dve.wait_ge(probs_ready, 8 * g + 4 * n + 4)
                two = slice(2 - 2 * n, 4 - 2 * n)
                dve.reciprocal(rsums[:, two, :], sums[:, two, :]).then_inc(rsums_ready, 1)
                dve.wait_ge(rsums_ready, 2 * g + n + 1)
                dve.wait_ge(y_psum, 8 * g + 4 * n + 4)
                for h in range(2):
                    for k in range(2):
                        i = 3 - 2 * n - k
                        at = (k * 2 + h) * C
                        r1 = x_sb[:, tile0 + i, :]
                        if h:
                            dve.wait_ge(y_added, 8 * g + 4 * n + k + 2)
                        dve.scalar_tensor_tensor(out=r1, in0=y_bank[n][:, at:at + C], scalar=rsums[:, i, h:h + 1],
                                                 in1=r1, op0=ALU.mult, op1=ALU.add).then_inc(y_added, 1)

            def step(g, tile0):
                neg_max(g, 0, 0, 3)
                neg_max(g, 1, 1, 2)
                copy_u(g)
                copy_tr(g, 1, 0, pT[:, 0, :], slice(0, S))
                neg_max(g, 2, 0, 1)
                copy_tr(g, 3, 0, pT[:, 2, 0:3 * P], slice(0, 3 * P))
                neg_max(g, 3, 1, 0)
                add_y(g, 0, tile0)
                split_g(g + 1)
                add_y(g, 1, tile0)

            with dve.Fori(0, B) as b:
                with dve.Fori(0, PAIRS) as p:
                    step(b * PAIRS + p, b * NT)
                wait_for(y_added, 8 * PAIRS * (b + 1) + 1, 0)
                for i in range(NT):
                    dve.bn_stats(stats[:, i, :], x_sb[:, b * NT + i, :]).then_inc(stats_ready, 1)
                wait_for(stats_ready, b * NT + NT, 1)
                for i in range(NT):
                    last = dve.bn_aggr(aggr[:, i, :], stats[:, i, :])
                last.then_inc(aggr_ready, 1)
                dve.wait_ge(aggr_ready, b + 1)
                dve.tensor_copy(meanvar[:, bass.ds(b * NT, NT), :], aggr[:, :, :]).then_inc(meanvar_ready, 1)


            def hi_products(src, dst, k, bc, experts, done, spread_at=None):
                for e in experts:
                    if spread_at is not None:
                        dve.wait_ge(spread_ready, spread_at + e + 1)
                    dve.tensor_tensor(dst[:, e, :], src[:, :].bitcast(F32), spread[:, bc, e, :], ALU.mult
                                      ).then_inc(done, 1)

            def choose(k):
                dve.wait_ge(logits_psum, k + 1)
                dve.tensor_tensor(logits[:, :, :], logits_bank[:, 0:NT * E].rearrange("p (t e) -> p t e", e=E),
                                  bg_sb[:, :].unsqueeze(1).broadcast_to([P, NT, E]), ALU.add).then_inc(argmax_step, 1)
                dve.wait_ge(argmax_step, 5 * k + 1)
                dve.tensor_reduce(best[:, :], logits[:, :, :], AX.X, ALU.max).then_inc(argmax_step, 1)
                dve.wait_ge(argmax_step, 5 * k + 2)
                dve.tensor_tensor(ranked[:, :, :], logits[:, :, :], best[:, :].unsqueeze(2).broadcast_to([P, NT, E]),
                                  ALU.is_equal).then_inc(argmax_step, 1)
                dve.wait_ge(argmax_step, 5 * k + 3)
                dve.tensor_tensor(ranked[:, :, :], ranked[:, :, :], rank[:, :].unsqueeze(1).broadcast_to([P, NT, E]),
                                  ALU.mult).then_inc(argmax_step, 1)
                dve.wait_ge(argmax_step, 5 * k + 4)
                dve.tensor_reduce(best[:, :], ranked[:, :, :], AX.X, ALU.max).then_inc(argmax_step, 1)
                dve.wait_ge(argmax_step, 5 * k + 5)
                dve.tensor_tensor(chosen[:, :, :], ranked[:, :, :], best[:, :].unsqueeze(2).broadcast_to([P, NT, E]),
                                  ALU.is_equal).then_inc(chosen_ready, 1)

            def slots(g, parity):
                if live(g + 1):
                    dve.wait_ge(x1T_rounded, g + 2)
                    if not first(g + 1):
                        dve.wait_ge(m1_pool, (g + 1) * E)
                    dve.tensor_tensor(x1T_lo[:, :], x1T_bank[:, :], x1T_hi[:, :].bitcast(F32), ALU.subtract
                                      ).then_inc(x1T_split, 1)
                if live(g - 1):
                    dve.wait_ge(h_rounded, g)
                    if not first(g - 1):
                        dve.wait_ge(m2_pool, (g - 1) * E)
                    dve.tensor_tensor(h_lo[:, :], h_32[:, :], h_hi[:, :].bitcast(F32), ALU.subtract
                                      ).then_inc(h_split, 1)
                    if not first(g - 1):
                        dve.wait_ge(yT_psum, g - 1)
                    hi_products(h_hi, m2_hi, g - 1, 1 - parity, range(0, 3), m2_dve)
                if live(g + 1):
                    choose(g + 1)
                if live(g - 1):
                    hi_products(h_hi, m2_hi, g - 1, 1 - parity, range(3, 6), m2_dve)
                if live(g - 2):
                    if not first(g - 2):
                        dve.wait_ge(out_ready, g - 2)
                    dve.wait_ge(x1_kept, 16 * (g - 1))
                    dve.wait_ge(back_psum, g - 1)
                    dve.tensor_tensor(r2[:, :, :], back_bank[:, :].rearrange("p (t c) -> p t c", c=C),
                                      x_sb[:, bass.ds((g - 2) * NT, NT), :], ALU.add).then_inc(r2_ready, 1)
                    wait_for(r2_ready, g - 1, 2)
                    for i in range(NT):
                        dve.bn_stats(stats[:, i, :], r2[:, i, :]).then_inc(r2_stats, 1)
                    wait_for(r2_stats, (g - 1) * NT, 3)
                    for i in range(NT):
                        last = dve.bn_aggr(aggr[:, i, :], stats[:, i, :])
                    last.then_inc(r2_aggr, 1)
                if live(g - 1):
                    hi_products(h_hi, m2_hi, g - 1, 1 - parity, range(6, E), m2_dve)
                if live(g + 1):
                    wait_for(chosenT_psum, g + 2, 4)
                    dve.tensor_copy(chosenT[:, bass.ds(g + 1, 1), :].rearrange("e n s -> e (n s)"),
                                    chosenT_bank[0:E, :]).then_inc(chosenT_ready, 1)
                    if not first(g + 1):
                        dve.wait_ge(h_psum, g + 1)
                    hi_products(x1T_hi, m1_hi, g + 1, 1 - parity, range(0, 4), m1_dve, (g + 1) * E)
                if live(g + 2):
                    if not first(g + 2):
                        dve.wait_ge(x1T_psum, g + 2)
                        dve.wait_ge(x1_kept, 16 * (g + 2))
                    for i in range(NT):
                        tile = (g + 2) * NT + i
                        last = dve.tensor_scalar(x1_now[:, i, :], x_sb[:, bass.ds(tile, 1), :].rearrange("p n c -> p (n c)"),
                                                 meanvar[:, bass.ds(tile, 1), 0], rstd1[:, bass.ds(tile, 1)],
                                                 ALU.subtract, ALU.mult)
                    last.then_inc(x1_ready, 1)
                if live(g + 1):
                    hi_products(x1T_hi, m1_hi, g + 1, 1 - parity, range(4, 6), m1_dve, (g + 1) * E)
                if live(g - 2):
                    dve.wait_ge(rstd2_ready, g - 1)
                    if not first(g - 2):
                        dve.wait_ge(stored, 16 * (g - 2))
                    for i in range(NT):
                        last = dve.tensor_scalar(out_sb[:, i, :], r2[:, i, :], aggr[:, i, 0:1], rstd2[:, i:i + 1],
                                                 ALU.subtract, ALU.mult)
                    last.then_inc(out_ready, 1)
                if live(g + 1):
                    hi_products(x1T_hi, m1_hi, g + 1, 1 - parity, range(6, E), m1_dve, (g + 1) * E)

            dve.wait_ge(bg_loaded, 16)
            dve.wait_ge(rstd1_ready, 2)
            expert_slots(dve, slots)


def kernel(**inputs):
    import numpy as _np
    import concourse.bacc as _bacc
    from concourse import mybir as _mybir
    from concourse.bass_utils import run_bass_kernel_spmd as _run

    a = {k[3:]: _np.asarray(v) for k, v in inputs.items()}
    x = a["attn_x"]
    B, S, C = x.shape
    H, D, _ = a["attn_w_q"].shape
    E = a["ffn_W1"].shape[0]
    pairs = H * D // 128
    arrays = {
        "x": x.reshape(B * S, C),
        "xT": x.transpose(0, 2, 1),
        "wq": a["attn_w_q"].reshape(pairs, 128, C),
        "wk": a["attn_w_k"].reshape(pairs, 128, C),
        "wv": a["attn_w_v"].reshape(pairs, 128, C),
        "wo": a["attn_w_o"].reshape(pairs, 128, C),
        "Wg": a["ffn_Wg"],
        "bg": a["ffn_bg"].reshape(1, E),
        "W1": a["ffn_W1"].transpose(1, 0, 2),
        "W2": a["ffn_W2"].transpose(1, 0, 2),
        "b12": _np.concatenate([a["ffn_b1"], a["ffn_b2"]], axis=1),
    }
    arrays = {f"in_{k}": _np.ascontiguousarray(v) for k, v in arrays.items()}
    nc = _bacc.Bacc("TRN2", target_bir_lowering=False, num_devices=1)
    args = [nc.dram_tensor(k, v.shape, _mybir.dt.from_np(v.dtype), kind="ExternalInput").ap() for k, v in arrays.items()]
    out = nc.dram_tensor("out", (B * S, C), _mybir.dt.float32, kind="ExternalOutput").ap()
    layer(nc, *args, out)
    r = _run(nc, [arrays], core_ids=[0])
    return r.results[0]["out"].reshape(B, S, C)
```

```python
from contextlib import ExitStack

import concourse.bass as bass
from concourse import mybir

F32 = mybir.dt.float32
F32R = mybir.dt.float32r
BF16 = mybir.dt.bfloat16
ACT = mybir.ActivationFunctionType
ALU = mybir.AluOpType
AX = mybir.AxisListType

P = 128
MASKED = -1e30
LN_EPS = 1e-5


def layer(nc, x, xT, wq, wk, wv, wo, Wg, bg, W1, W2, b12, out):
    B, C, S = xT.shape
    PAIRS = wq.shape[0]
    E = Wg.shape[1]
    D = P // 2
    NT = S // P
    TILES = B * NT
    STEPS = B * PAIRS
    QSCALE = float(D) ** -0.5
    SUMMED = 3
    PICKED = E - SUMMED
    assert C == P and NT == 4

    with ExitStack() as ctx:
        def sb(name, shape, dt):
            return ctx.enter_context(nc.sbuf_tensor(name, shape, dt))

        def sem(name):
            return ctx.enter_context(nc.semaphore(name))

        x_sb = sb("x_sb", [P, TILES, C], F32)
        meanvar = sb("meanvar", [P, TILES, 2], F32)
        rstd1 = sb("rstd1", [P, TILES], F32)
        ident = sb("ident", [P, P], F32)
        zeros = sb("zeros", [P, E * P], F32)
        carrier = sb("carrier", [P, 16], F32)
        eps = sb("eps", [P, TILES], F32)
        minus_half = sb("minus_half", [P, TILES], F32)
        stats = sb("stats", [P, NT, 6], F32)
        aggr = sb("aggr", [P, NT, 2], F32)
        w1_hi = sb("w1_hi", [P, E, P], F32R)
        w1_lo = sb("w1_lo", [P, E, P], F32R)
        w2_hi = sb("w2_hi", [P, E, P], F32R)
        w2_lo = sb("w2_lo", [P, E, P], F32R)
        w1_raw = sb("w1_raw", [P, E, P], F32)
        w2_raw = sb("w2_raw", [P, E, P], F32)
        wg_raw = sb("wg_raw", [P, E], F32)
        wg_halves = sb("wg_halves", [P, 2, E], F32R)
        bg_sb = sb("bg_sb", [P, E], F32)
        b_raw = sb("b_raw", [E, 2 * P], F32)
        b_halves = sb("b_halves", [E, 2, 2 * P], F32R)
        rank = sb("rank", [P, E], F32)
        pick_raw = sb("pick_raw", [E, E, P], F32)
        pick = sb("pick", [E, E, P], F32R)

        attn = ctx.enter_context(ExitStack())

        def sb1(name, shape, dt):
            return attn.enter_context(nc.sbuf_tensor(name, shape, dt))

        xT_32 = sb1("xT_32", [P, B, S], F32)
        xT_hi = sb1("xT_hi", [P, B, S], F32R)
        xT_lo = sb1("xT_lo", [P, B, S], F32R)
        xT_now = sb1("xT_now", [P, 2, S], F32R)
        wqk_halves = sb1("wqk_halves", [P, PAIRS, 2, 2, C], F32R)
        wqk_now = sb1("wqk_now", [P, 2, 2, C], F32R)
        wvo_hi = sb1("wvo_hi", [P, PAIRS, 2 * C], F32R)
        wvo_lo = sb1("wvo_lo", [P, PAIRS, 2 * C], F32R)
        ident_bf = sb1("ident_bf", [P, P], BF16)
        mask_bf = sb1("mask_bf", [P, P], BF16)
        g_32 = sb1("g_32", [P, 2, S], F32)
        g_hi = sb1("g_hi", [P, 2, S], F32R)
        g_lo = sb1("g_lo", [P, 2, S], F32R)
        u_sb = sb1("u_sb", [P, NT, 2 * C], F32)
        negmax = sb1("negmax", [P, NT, 2], F32)
        sums = sb1("sums", [P, NT, 2], F32)
        rsums = sb1("rsums", [P, NT, 2], F32)
        with ExitStack() as setup:
            def sb0(name, shape, dt):
                return setup.enter_context(nc.sbuf_tensor(name, shape, dt))

            wq_sb = sb0("wq_sb", [P, PAIRS, C], F32)
            wk_sb = sb0("wk_sb", [P, PAIRS, C], F32)
            wqk_raw = sb0("wqk_raw", [P, PAIRS, 2, C], F32)
            wv_sb = sb0("wv_sb", [P, PAIRS, C], F32)
            wo_sb = sb0("wo_sb", [P, PAIRS, C], F32)
            wvo_raw = sb0("wvo_raw", [P, PAIRS, 2 * C], F32)
        probs = sb1("probs", [P, 2, 2, S], F32)
        pT = sb1("pT", [P, 6, S], F32)

        attn.close()
        x1_now = sb("x1_now", [P, NT, C], F32)
        x1T_hi = sb("x1T_hi", [P, 2, S], F32R)
        x1T_lo = sb("x1T_lo", [P, 2, S], F32R)
        logits = sb("logits", [P, NT, E], F32)
        best = sb("best", [P, NT], F32)
        ranked = sb("ranked", [P, NT, E], F32)
        chosen = sb("chosen", [P, NT, E], F32)
        chosenT = sb("chosenT", [E, B, S], F32R)
        spread = sb("spread", [P, 2, E, S], BF16)
        m1_hi = sb("m1_hi", [P, SUMMED, S], F32R)
        m1_lo = sb("m1_lo", [P, SUMMED, S], F32R)
        m2_hi = sb("m2_hi", [P, SUMMED, S], F32R)
        m2_lo = sb("m2_lo", [P, SUMMED, S], F32R)
        h_pick = sb("h_pick", [P, S], F32)
        h_32 = sb("h_32", [P, S], F32)
        h_hi = sb("h_hi", [P, 2, S], F32R)
        h_lo = sb("h_lo", [P, 2, S], F32R)
        yT_sb = sb("yT_sb", [P, S], F32)
        r2 = sb("r2", [P, NT, C], F32)
        rstd2 = sb("rstd2", [P, NT], F32)
        shift2 = sb("shift2", [P, NT], F32)
        out_sb = sb("out_sb", [P, NT, C], F32)

        bank = [ctx.enter_context(nc.psum_tensor(f"bank{i}", [P, S], F32)) for i in range(8)]
        s_bank = [[bank[0], bank[1]], [bank[2], bank[3]]]
        t_bank = [bank[4], bank[5]]
        y_bank = [bank[6], bank[7]]

        x1T_bank = back_bank = bank[0]
        logits_bank = chosenT_bank = bank[1]
        spread_bank = [bank[2], bank[3]]
        sum_bank = bank[4]
        pick_bank = [bank[5], bank[6], bank[7]]

        def live(g):
            return not isinstance(g, int) or 0 <= g < B

        def first(g):
            return isinstance(g, int) and g == 0

        def expert_slots(engine, slots):
            for g in range(-2, 2):
                slots(g, g % 2)
            with engine.Fori(1, B // 2 - 1) as half:
                for parity in range(2):
                    slots(half * 2 + parity, parity)
            for g in range(B - 2, B + 2):
                slots(g, g % 2)

        x_loaded = sem("x_loaded")
        wq_loaded = sem("wq_loaded")
        wk_loaded = sem("wk_loaded")
        wv_loaded = sem("wv_loaded")
        wo_loaded = sem("wo_loaded")
        xT_loaded = sem("xT_loaded")
        wqk_moved = sem("wqk_moved")
        pool_zero = sem("pool_zero")
        consts_ready = sem("consts_ready")
        xT_split = sem("xT_split")
        xT_moved = sem("xT_moved")
        wqk_psum = sem("wqk_psum")
        wqk_copied = sem("wqk_copied")
        wqk_split = sem("wqk_split")
        wvo_split = sem("wvo_split")
        half_xT = sem("half_xT")
        half_wqk = sem("half_wqk")
        half_wvo = sem("half_wvo")
        g_psum = sem("g_psum")
        u_psum = sem("u_psum")
        g_rounded = sem("g_rounded")
        u_copied_act = sem("u_copied_act")
        u_copied_dve = sem("u_copied_dve")
        wvo_psum = sem("wvo_psum")
        wvo_copied = sem("wvo_copied")
        g_split = sem("g_split")
        g_joined = sem("g_joined")
        scores_ready = sem("scores_ready")
        negmax_ready = sem("negmax_ready")
        probs_ready = sem("probs_ready")
        tr_psum = sem("tr_psum")
        tr_dve = sem("tr_dve")
        tr_act = sem("tr_act")
        y_psum = sem("y_psum")
        rsums_ready = sem("rsums_ready")
        y_added = sem("y_added")
        stats_ready = sem("stats_ready")
        aggr_ready = sem("aggr_ready")
        meanvar_ready = sem("meanvar_ready")
        w_loaded = sem("w_loaded")
        bg_loaded = sem("bg_loaded")
        b_loaded = sem("b_loaded")
        w_rounded = sem("w_rounded")
        w_split = sem("w_split")
        small_raw = sem("small_raw")
        small_rounded = sem("small_rounded")
        small_split = sem("small_split")
        var1_ready = sem("var1_ready")
        var2_ready = sem("var2_ready")
        pow2_ready = sem("pow2_ready")
        rstd1_ready = sem("rstd1_ready")
        x1_ready = sem("x1_ready")
        x1_kept = sem("x1_kept")
        x1T_psum = sem("x1T_psum")
        x1T_rounded = sem("x1T_rounded")
        x1T_split = sem("x1T_split")
        logits_psum = sem("logits_psum")
        logits_ready = sem("logits_ready")
        argmax_step = sem("argmax_step")
        chosen_ready = sem("chosen_ready")
        chosenT_psum = sem("chosenT_psum")
        chosenT_ready = sem("chosenT_ready")
        spread_psum = sem("spread_psum")
        spread_ready = sem("spread_ready")
        m1_ready = sem("m1_ready")
        h_outs = sem("h_outs")
        h_picked = sem("h_picked")
        h_psum = sem("h_psum")
        h_summed = sem("h_summed")
        h_ready = sem("h_ready")
        h_rounded = sem("h_rounded")
        h_split = sem("h_split")
        m2_ready = sem("m2_ready")
        y_outs = sem("y_outs")
        y_picked = sem("y_picked")
        yT_psum = sem("yT_psum")
        yT_summed = sem("yT_summed")
        back_psum = sem("back_psum")
        r2_ready = sem("r2_ready")
        r2_stats = sem("r2_stats")
        r2_aggr = sem("r2_aggr")
        rstd2_ready = sem("rstd2_ready")
        out_ready = sem("out_ready")
        stored = sem("stored")

        block = ctx.enter_context(nc.Block())

        @block.sync
        def _(sp):
            sp.dma_start(wq_sb[:, :, :], wq.rearrange("a p c -> p a c")).then_inc(wq_loaded, 16)
            sp.dma_start(wk_sb[:, :, :], wk.rearrange("a p c -> p a c")).then_inc(wk_loaded, 16)
            sp.dma_start(xT_32[:, :, :], xT.rearrange("b c s -> c b s")).then_inc(xT_loaded, 16)
            sp.dma_start(wv_sb[:, :, :], wv.rearrange("a p c -> p a c")).then_inc(wv_loaded, 16)
            sp.dma_start(wo_sb[:, :, :], wo.rearrange("a p c -> p a c")).then_inc(wo_loaded, 16)
            sp.dma_start(x_sb[:, :, :], x.rearrange("(t p) c -> p t c", p=P)).then_inc(x_loaded, 16)
            sp.dma_start(w1_raw[:, :, :], W1).then_inc(w_loaded, 16)
            sp.dma_start(w2_raw[:, :, :], W2).then_inc(w_loaded, 16)
            sp.dma_start(wg_raw[:, :], Wg).then_inc(w_loaded, 16)
            sp.dma_start(bg_sb[:, :], bg.broadcast_to([P, E])).then_inc(bg_loaded, 16)
            sp.dma_start(b_raw[:, :], b12).then_inc(w_loaded, 16)

            def move_wqk(pair):
                sp.dma_start(wqk_now[:, :, :, :].rearrange("p a h c -> p (a h c)").bitcast(F32),
                             wqk_halves[:, bass.ds(pair, 1), :, :, :].rearrange("p n a h c -> p (n a h c)").bitcast(F32)
                             ).then_inc(wqk_moved, 16)

            def next_wqk(n, pair):
                sp.wait_ge(g_psum, 2 * n)
                move_wqk(pair)

            def move_xT(b):
                for half, src in enumerate((xT_hi, xT_lo)):
                    sp.dma_start(xT_now[:, half, :].bitcast(F32),
                                 src[:, bass.ds(b, 1), :].rearrange("p n s -> p (n s)").bitcast(F32)
                                 ).then_inc(xT_moved, 16)

            sp.wait_ge(wqk_split, 1)
            move_wqk(0)
            sp.wait_ge(xT_split, B)
            move_xT(0)
            with sp.Fori(0, B - 1) as b:
                with sp.Fori(0, PAIRS - 1) as p:
                    next_wqk(b * PAIRS + p + 1, p + 1)
                next_wqk(b * PAIRS + PAIRS, 0)
                sp.wait_ge(u_psum, b * PAIRS + PAIRS)
                move_xT(b + 1)
            with sp.Fori(0, PAIRS - 1) as p:
                next_wqk((B - 1) * PAIRS + p + 1, p + 1)
            next_wqk(B * PAIRS, 0)

            def keep_x1(g):
                sp.wait_ge(x1_ready, g + 1)
                sp.dma_start(x_sb[:, bass.ds(g * NT, NT), :], x1_now[:, :, :]).then_inc(x1_kept, 16)

            def store(g):
                sp.wait_ge(out_ready, g + 1)
                sp.dma_start(out_groups[bass.ds(g, 1)].rearrange("n p t c -> (n p) t c"), out_sb[:, :, :]
                             ).then_inc(stored, 16)

            out_groups = out.rearrange("(g t p) c -> g p t c", p=P, t=NT)
            for g in range(4):
                keep_x1(g)
            with sp.Fori(4, B) as g:
                keep_x1(g)
                store(g - 4)
            for g in range(B - 4, B):
                store(g)
            sp.wait_ge(stored, 16 * B)

        @block.gpsimd
        def _(pool):
            pool.memset(ident[:, :], 0.0).then_inc(pool_zero, 1)
            pool.memset(ident_bf[:, :], 0.0).then_inc(pool_zero, 1)
            pool.memset(mask_bf[:, :], 0.0).then_inc(pool_zero, 1)
            pool.memset(zeros[:, :], 0.0).then_inc(pool_zero, 1)
            pool.wait_ge(pool_zero, 4)
            for t in (ident, ident_bf):
                pool.affine_select(out=t[:, :], in_=t[:, :], compare_op=ALU.not_equal, fill=1.0, base=0,
                                   pattern=[[-1, P]], channel_multiplier=1).then_inc(consts_ready, 1)
            pool.affine_select(out=mask_bf[:, :], in_=mask_bf[:, :], compare_op=ALU.is_ge, fill=MASKED, base=0,
                               pattern=[[-1, P]], channel_multiplier=1).then_inc(consts_ready, 1)

            pool.wait_ge(xT_loaded, 16)
            for b in range(B):
                pool.tensor_tensor(xT_hi[:, b, :], xT_32[:, b, :], zeros[:, 0:S], ALU.add).then_inc(half_xT, 1)
            for b in range(B):
                pool.wait_ge(half_xT, b + 1)
                pool.tensor_tensor(xT_lo[:, b, :], xT_32[:, b, :], xT_hi[:, b, :].bitcast(F32), ALU.subtract
                                   ).then_inc(xT_split, 1)

            def join_g(n):
                pool.wait_ge(g_split, 2 * n + 2)
                pool.tensor_tensor(g_32[:, :, :], g_hi[:, :, :].bitcast(F32), g_lo[:, :, :].bitcast(F32), ALU.add
                                   ).then_inc(g_joined, 1)

            join_g(0)
            for e in range(E):
                pool.memset(rank[:, e:e + 1], float(E - e)).then_inc(small_raw, 1)
            pool.memset(pick_raw[:, :, :], 0.0).then_inc(small_raw, 1)
            pool.memset(eps[:, :], LN_EPS).then_inc(small_raw, 1)
            pool.memset(minus_half[:, :], -0.5).then_inc(small_raw, 1)
            pool.wait_ge(small_raw, E + 3)
            pool.affine_select(out=pick_raw[:, :, :], in_=pick_raw[:, :, :], compare_op=ALU.not_equal, fill=1.0,
                               base=0, pattern=[[-1, E], [0, P]], channel_multiplier=1).then_inc(small_raw, 1)
            pool.wait_ge(small_raw, E + 4)
            pool.tensor_tensor(pick[:, :, :].rearrange("k e p -> k (e p)"),
                               pick_raw[:, :, :].rearrange("k e p -> k (e p)"), zeros[0:E, :], ALU.add).then_inc(small_rounded, 1)
            pool.wait_ge(w_loaded, 64)
            flat = [t[:, :, :].rearrange("p e i -> p (e i)") for t in (w1_raw, w1_hi, w1_lo, w2_raw, w2_hi, w2_lo)]
            parts = (flat[0:3], flat[3:6], (wg_raw[:, :], wg_halves[:, 0, :], wg_halves[:, 1, :]),
                     (b_raw[:, :], b_halves[:, 0, :], b_halves[:, 1, :]))
            for raw, hi, lo in parts:
                pool.tensor_tensor(hi, raw, zeros[0:raw.shape[0], 0:raw.shape[1]], ALU.add).then_inc(w_rounded, 1)
            pool.wait_ge(w_rounded, 4)
            for raw, hi, lo in parts:
                pool.tensor_tensor(lo, raw, hi.bitcast(F32), ALU.subtract).then_inc(w_split, 1)

            def joins(b):
                with pool.Fori(0, PAIRS) as p:
                    join_g(b * PAIRS + p + 1)

            def first_rstd(tiles, batches):
                pool.wait_ge(meanvar_ready, batches)
                n = tiles.stop - tiles.start
                pool.tensor_tensor(rstd1[:, tiles], meanvar[:, tiles, 1], eps[:, 0:n], ALU.add).then_inc(var1_ready, 1)
                pool.wait_ge(var1_ready, batches - B + 2)
                pool.tensor_tensor(rstd1[:, tiles], rstd1[:, tiles], minus_half[:, 0:n], ALU.pow
                                   ).then_inc(rstd1_ready, 1)

            with pool.Fori(0, B - 1) as b:
                joins(b)
            first_rstd(slice(0, TILES - NT), B - 1)
            joins(B - 1)
            first_rstd(slice(TILES - NT, TILES), B)

            def products(src, dst, mask, done, spread_at=None):
                for e in range(SUMMED):
                    if spread_at is not None:
                        pool.wait_ge(spread_ready, spread_at + e + 1)
                    for half in range(2):
                        pool.tensor_tensor(dst[half][:, e, :], src[half], mask[:, e, :], ALU.mult).then_inc(done, 1)

            def slots(g, parity):
                if live(g - 2):
                    pool.wait_ge(r2_aggr, g - 1)
                    pool.tensor_tensor(rstd2[:, :], aggr[:, :, 1], eps[:, 0:NT], ALU.add).then_inc(var2_ready, 1)
                    pool.tensor_tensor(shift2[:, :], zeros[:, 0:NT], aggr[:, :, 0], ALU.subtract).then_inc(var2_ready, 1)
                    pool.wait_ge(var2_ready, 2 * (g - 1))
                    pool.tensor_tensor(rstd2[:, :], rstd2[:, :], minus_half[:, 0:NT], ALU.pow).then_inc(pow2_ready, 1)
                    pool.wait_ge(pow2_ready, g - 1)
                    pool.tensor_tensor(shift2[:, :], shift2[:, :], rstd2[:, :], ALU.mult).then_inc(rstd2_ready, 1)
                if live(g + 1):
                    pool.wait_ge(x1T_split, g + 2)
                    if not first(g + 1):
                        pool.wait_ge(h_psum, g + 1)
                    products((x1T_hi[:, 1 - parity, :].bitcast(F32), x1T_lo[:, 1 - parity, :].bitcast(F32)),
                             (m1_hi, m1_lo), spread[:, 1 - parity, :, :], m1_ready, (g + 1) * E)
                if live(g):
                    pool.wait_ge(h_split, g + 1)
                    if not first(g):
                        pool.wait_ge(yT_psum, g)
                    products((h_hi[:, parity, :].bitcast(F32), h_lo[:, parity, :].bitcast(F32)), (m2_hi, m2_lo),
                             spread[:, parity, :, :], m2_ready)

            expert_slots(pool, slots)

        @block.tensor
        def _(pe):
            def three(out_ap, a_hi, a_lo, b_hi, b_lo, **last):
                pe.matmul(out_ap, a_lo, b_hi, start=True, stop=False)
                pe.matmul(out_ap, a_hi, b_lo, start=False, stop=False)
                return pe.matmul(out_ap, a_hi, b_hi, start=False, stop=True)

            def batch_of(t, b, w=slice(0, S)):
                return t[:, bass.ds(b, 1), w].rearrange("p n s -> p (n s)")

            def project_g(n, b):
                pe.wait_ge(wqk_moved, 16 * (n + 1))
                for h in range(2):
                    three(s_bank[0][h][:, :], wqk_now[:, 0, h, :], wqk_now[:, 1, h, :], batch_of(xT_hi, b),
                          batch_of(xT_lo, b)).then_inc(g_psum, 1)

            def project_u(pair, b):
                pe.wait_ge(xT_moved, 32 * b + 32)
                for j in range(NT):
                    t = slice(j * P, (j + 1) * P)
                    c = slice(j % 2 * 2 * C, (j % 2 + 1) * 2 * C)
                    last = three(y_bank[j // 2][:, c], xT_now[:, 0, t], xT_now[:, 1, t], wvo_hi[:, pair, :],
                                 wvo_lo[:, pair, :])
                last.then_inc(u_psum, 1)

            def scores(slot, i, b, g=None):
                w = (i + 1) * P
                t = slice(i * P, w)
                parts = ((g_lo, xT_hi), (g_hi, xT_lo), (g_hi, xT_hi)) if i else ((g_32, xT_32),)
                for h in range(2):
                    if g is not None:
                        pe.wait_ge(g_split, 2 * g + h + 1)
                    for n, (a, c) in enumerate(parts):
                        pe.matmul(s_bank[slot][h][:, 0:w], a[:, h, t], batch_of(c, b, slice(0, w)), start=(n == 0), stop=False)
                    pe.matmul(s_bank[slot][h][:, t], ident_bf[:, :], mask_bf[:, :], start=False, stop=True
                              ).then_inc(scores_ready, 1)

            def transposes(use, slot, blocks):
                for n, (h, j) in enumerate(blocks):
                    last = pe.transpose(t_bank[use % 2][:, n * P:(n + 1) * P], probs[:, slot, h, j * P:(j + 1) * P],
                                        ident[:, :])
                last.then_inc(tr_psum, 1)

            def pu(use, i, h, first=0):
                at = ((3 - i) % 2 * 2 + h) * C
                for j in range(i + 1):
                    last = pe.matmul(y_bank[(3 - i) // 2][:, at:at + C],
                                     pT[:, use, (first + j) * P:(first + j + 1) * P],
                                     u_sb[:, j, h * C:(h + 1) * C], start=(j == 0), stop=(j == i))
                last.then_inc(y_psum, 1)

            def step(g, p, b, b_next):
                scores(0, 3, b, g)
                scores(1, 2, b)
                pe.wait_ge(y_added, 8 * g + 1)
                project_u(p, b)
                pe.wait_ge(probs_ready, 8 * g + 1)
                transposes(0, 0, [(0, j) for j in range(4)])
                pe.wait_ge(probs_ready, 8 * g + 2)
                transposes(1, 0, [(1, j) for j in range(4)])
                scores(0, 1, b)
                pe.wait_ge(u_copied_act, g + 1)
                pe.wait_ge(u_copied_dve, g + 1)
                pe.wait_ge(tr_dve, 2 * g + 1)
                pu(0, 3, 0)
                pe.wait_ge(tr_act, 4 * g + 1)
                pu(1, 3, 1)
                pe.wait_ge(probs_ready, 8 * g + 3)
                transposes(2, 1, [(0, j) for j in range(3)])
                pe.wait_ge(probs_ready, 8 * g + 4)
                transposes(3, 1, [(1, j) for j in range(3)])
                pe.wait_ge(g_joined, g + 1)
                scores(1, 0, b)
                pe.wait_ge(probs_ready, 8 * g + 6)
                pe.wait_ge(tr_dve, 2 * g + 2)
                transposes(4, 0, [(h, j) for h in range(2) for j in range(2)])
                pu(2, 2, 0)
                pe.wait_ge(tr_act, 4 * g + 2)
                pu(3, 2, 1)
                pe.wait_ge(probs_ready, 8 * g + 8)
                transposes(5, 1, [(0, 0), (1, 0)])
                project_g(g + 1, b_next)
                pe.wait_ge(tr_act, 4 * g + 3)
                pu(4, 1, 0)
                pu(4, 1, 1, first=2)
                pe.wait_ge(tr_act, 4 * g + 4)
                pu(5, 0, 0)
                pu(5, 0, 1, first=1)

            def weight_products(a, c, banks, done):
                for n in range(2 * PAIRS):
                    r = slice(n % 2 * D, (n % 2 + 1) * D)
                    m = n // 2 % 4
                    last = pe.matmul(banks[n % 2 * 2 + n // 8][:, m * C:(m + 1) * C], a[r, n // 2, :], c[r, n // 2, :],
                                     start=True, stop=True)
                last.then_inc(done, 1)

            pe.wait_ge(wq_loaded, 16)
            pe.wait_ge(wk_loaded, 16)
            weight_products(wq_sb, wk_sb, bank[0:4], wqk_psum)
            pe.wait_ge(wv_loaded, 16)
            pe.wait_ge(wo_loaded, 16)
            weight_products(wv_sb, wo_sb, bank[4:8], wvo_psum)
            pe.wait_ge(wqk_split, 1)
            pe.wait_ge(xT_split, B)
            project_g(0, 0)
            pe.wait_ge(consts_ready, 3)
            pe.wait_ge(wvo_split, 1)
            with pe.Fori(0, B - 1) as b:
                with pe.Fori(0, PAIRS - 1) as p:
                    step(b * PAIRS + p, p, b, b)
                step(b * PAIRS + PAIRS - 1, PAIRS - 1, b, b + 1)
            with pe.Fori(0, PAIRS) as p:
                step((B - 1) * PAIRS + p, p, B - 1, B - 1)

            def slots(g, parity):
                def chosen_of(k):
                    return chosenT[:, bass.ds(k, 1), :].rearrange("e n s -> e (n s)")

                def expert(out_bank, w, e, m, **when):
                    (w_hi, w_lo), (m_hi, m_lo) = w, m
                    pe.matmul(out_bank[:, :], w_hi[:, e, :], m_lo, start=when["start"], stop=False)
                    pe.matmul(out_bank[:, :], w_lo[:, e, :], m_hi, start=False, stop=False)
                    return pe.matmul(out_bank[:, :], w_hi[:, e, :], m_hi, start=False, stop=when["stop"])

                def bias(half_of, k):
                    pe.matmul(sum_bank[:, :], b_halves[:, 1, half_of], chosen_of(k), start=False, stop=False)
                    return pe.matmul(sum_bank[:, :], b_halves[:, 0, half_of], chosen_of(k), start=False, stop=True)

                def first_layer(picks):
                    for n in picks:
                        if n >= 3:
                            pe.wait_ge(h_picked, g * PICKED + n - 2)
                        elif not first(g) and not first(g - 1) and n == 0:
                            pe.wait_ge(y_picked, (g - 1) * PICKED)
                        expert(pick_bank[n % 3], (w1_hi, w1_lo), SUMMED + n,
                               (x1T_hi[:, parity, :], x1T_lo[:, parity, :]), start=True, stop=True).then_inc(h_outs, 1)

                def spread_choice(e):
                    pe.matmul(spread_bank[e % 2][:, :], pick[:, e, :], chosen_of(g + 1), start=True, stop=True
                              ).then_inc(spread_psum, 1)

                if live(g):
                    first_layer((0, 1, 2))
                if live(g + 1):
                    pe.wait_ge(x1T_split, g + 2)
                    for i in range(NT):
                        t = slice(i * P, (i + 1) * P)
                        last = three(logits_bank[:, i * E:(i + 1) * E], x1T_hi[:, 1 - parity, t],
                                     x1T_lo[:, 1 - parity, t], wg_halves[:, 0, :], wg_halves[:, 1, :])
                    last.then_inc(logits_psum, 1)
                if live(g):
                    first_layer((3,))
                if live(g - 2):
                    pe.wait_ge(yT_summed, g - 1)
                    for i in range(NT):
                        t = slice(i * P, (i + 1) * P)
                        last = pe.transpose(back_bank[:, t], yT_sb[:, t], ident[:, :])
                    last.then_inc(back_psum, 1)
                if live(g):
                    first_layer((4,))
                if live(g + 1):
                    pe.wait_ge(chosen_ready, g + 2)
                    for i in range(NT):
                        last = pe.transpose(chosenT_bank[0:E, i * P:(i + 1) * P], chosen[:, i, :], ident[:, :])
                    last.then_inc(chosenT_psum, 1)
                if live(g):
                    if not first(g) and not first(g - 1):
                        pe.wait_ge(yT_summed, g - 1)
                    for e in range(SUMMED):
                        pe.wait_ge(m1_ready, (g * SUMMED + e + 1) * 2)
                        expert(sum_bank, (w1_hi, w1_lo), e, (m1_hi[:, e, :], m1_lo[:, e, :]), start=(e == 0), stop=False)
                    bias(slice(0, P), g).then_inc(h_psum, 1)

                for n in range(E):
                    if live(g + 2) and n == 6:
                        pe.wait_ge(x1_ready, g + 3)
                        for i in range(NT):
                            last = pe.transpose(x1T_bank[:, i * P:(i + 1) * P], x1_now[:, i, :], ident[:, :])
                        last.then_inc(x1T_psum, 1)
                    if live(g + 1):
                        if n == 0:
                            pe.wait_ge(chosenT_ready, g + 2)
                        if n >= 2 or not first(g + 1):
                            pe.wait_ge(spread_ready, (g + 1) * E + n - 1)
                    if live(g - 1) and n < PICKED:
                        if n >= 3:
                            pe.wait_ge(y_picked, (g - 1) * PICKED + n - 2)
                        elif live(g) and n == 0:
                            pe.wait_ge(h_picked, (g + 1) * PICKED)
                        expert(pick_bank[n % 3], (w2_hi, w2_lo), SUMMED + n, (h_hi[:, 1 - parity, :], h_lo[:, 1 - parity, :]), start=True,
                               stop=True).then_inc(y_outs, 1)
                    elif live(g - 1):
                        e = n - PICKED
                        if live(g) and e == 0:
                            pe.wait_ge(h_summed, g + 1)
                        pe.wait_ge(m2_ready, ((g - 1) * SUMMED + e + 1) * 2)
                        expert(sum_bank, (w2_hi, w2_lo), e, (m2_hi[:, e, :], m2_lo[:, e, :]), start=(e == 0), stop=False)
                    if live(g + 1):
                        spread_choice(n)
                if live(g - 1):
                    bias(slice(P, 2 * P), g - 1).then_inc(yT_psum, 1)

            pe.wait_ge(w_split, 4)
            pe.wait_ge(small_rounded, 1)
            expert_slots(pe, slots)

        @block.scalar
        def _(act):
            def round_g(n):
                for h in range(2):
                    act.wait_ge(g_psum, 2 * n + h + 1)
                    act.activation(g_hi[:, h, :], s_bank[0][h][:, :], ACT.Copy).then_inc(g_rounded, 1)

            def copy_u(n):
                act.wait_ge(u_psum, n + 1)
                act.activation(u_sb[:, 0:2, :].rearrange("p a c -> p (a c)"), y_bank[0][:, :], ACT.Copy
                               ).then_inc(u_copied_act, 1)

            def exps(g, slot, i, h, wait):
                w = (i + 1) * P
                if wait:
                    act.wait_ge(negmax_ready, 5 * g + wait)
                act.activation(probs[:, slot, h, 0:w], s_bank[slot][h][:, 0:w], ACT.Exp,
                               bias=negmax[:, i, h:h + 1], accum_out=sums[:, i, h:h + 1]).then_inc(probs_ready, 1)

            def copy_tr(g, count, bank_no, dst, w):
                act.wait_ge(tr_psum, 6 * g + count)
                act.activation(dst, t_bank[bank_no][:, w], ACT.Copy).then_inc(tr_act, 1)

            round_g(0)
            with act.Fori(0, STEPS) as g:
                exps(g, 0, 3, 0, 1)
                exps(g, 0, 3, 1, 2)
                exps(g, 1, 2, 0, 3)
                copy_u(g)
                copy_tr(g, 2, 1, pT[:, 1, :], slice(0, S))
                exps(g, 1, 2, 1, 0)
                exps(g, 0, 1, 0, 4)
                exps(g, 0, 1, 1, 0)
                copy_tr(g, 4, 1, pT[:, 3, 0:3 * P], slice(0, 3 * P))
                exps(g, 1, 0, 0, 5)
                exps(g, 1, 0, 1, 0)
                copy_tr(g, 5, 0, pT[:, 4, :], slice(0, S))
                copy_tr(g, 6, 1, pT[:, 5, 0:2 * P], slice(0, 2 * P))
                round_g(g + 1)

            def slots(g, parity):
                for e in range(E):
                    if live(g) and e == 3:
                        act.wait_ge(h_summed, g + 1)
                        if not first(g):
                            act.wait_ge(h_split, g)
                        act.activation(h_32[:, :], h_pick[:, :], ACT.Gelu).then_inc(h_ready, 1)
                        act.wait_ge(h_ready, g + 1)
                        if not first(g) and not first(g - 1):
                            act.wait_ge(yT_psum, g - 1)
                        act.activation(h_hi[:, parity, :], h_32[:, :], ACT.Copy).then_inc(h_rounded, 1)
                    if live(g + 2) and e == 6:
                        act.wait_ge(x1T_psum, g + 3)
                        if live(g):
                            act.wait_ge(m1_ready, (g + 1) * SUMMED * 2)
                            act.wait_ge(h_psum, g + 1)
                        act.activation(x1T_hi[:, parity, :], x1T_bank[:, :], ACT.Copy).then_inc(x1T_rounded, 1)
                    if live(g + 1):
                        act.wait_ge(spread_psum, (g + 1) * E + e + 1)
                        if live(g - 1):
                            if e == 0:
                                act.wait_ge(m2_ready, g * SUMMED * 2)
                            if e >= SUMMED:
                                act.wait_ge(y_picked, (g - 1) * PICKED + e - SUMMED + 1)
                        act.activation(spread[:, 1 - parity, e, :], spread_bank[e % 2][:, :], ACT.Copy
                                       ).then_inc(spread_ready, 1)
                if live(g - 2):
                    act.wait_ge(rstd2_ready, g - 1)
                    if not first(g - 2):
                        act.wait_ge(stored, 16 * (g - 2))
                    for i in range(NT):
                        last = act.activation(out_sb[:, i, :], r2[:, i, :], ACT.Identity, bias=shift2[:, i:i + 1],
                                              scale=rstd2[:, i:i + 1])
                    last.then_inc(out_ready, 1)

            expert_slots(act, slots)

        @block.vector
        def _(dve):
            def split_g(n):
                for h in range(2):
                    dve.wait_ge(g_rounded, 2 * n + h + 1)
                    dve.tensor_tensor(g_lo[:, h, :], s_bank[0][h][:, :], g_hi[:, h, :].bitcast(F32), ALU.subtract
                                      ).then_inc(g_split, 1)

            def copy_u(n):
                dve.wait_ge(u_psum, n + 1)
                dve.tensor_copy(u_sb[:, 2:4, :].rearrange("p a c -> p (a c)"), y_bank[1][:, :]
                                ).then_inc(u_copied_dve, 1)

            def copy_tr(g, count, bank_no, dst, w):
                dve.wait_ge(tr_psum, 6 * g + count)
                dve.tensor_copy(dst, t_bank[bank_no][:, w]).then_inc(tr_dve, 1)

            def wait_for(signal, count, cell):
                dve.wait_ge(signal, count)
                dve.memset(carrier[:, cell:cell + 1], 0.0)

            dve.wait_ge(wqk_psum, 1)
            for n in range(4):
                h, m = n // 2, n % 2 * 4
                dve.tensor_scalar(wqk_raw[:, m:m + 4, h, :], bank[n][:, :].rearrange("p (a c) -> p a c", c=C),
                                  QSCALE, None, ALU.mult).then_inc(wqk_copied, 1)
            dve.wait_ge(wqk_copied, 4)
            dve.tensor_copy(wqk_halves[:, :, 0, :, :], wqk_raw[:, :, :, :]).then_inc(half_wqk, 1)
            dve.wait_ge(half_wqk, 1)
            dve.tensor_tensor(wqk_halves[:, :, 1, :, :], wqk_raw[:, :, :, :], wqk_halves[:, :, 0, :, :].bitcast(F32),
                              ALU.subtract).then_inc(wqk_split, 1)
            dve.wait_ge(wvo_psum, 1)
            for n in range(4):
                h, m = n // 2, n % 2 * 4
                dve.tensor_copy(wvo_raw[:, m:m + 4, h * C:(h + 1) * C],
                                bank[4 + n][:, :].rearrange("p (a c) -> p a c", c=C)).then_inc(wvo_copied, 1)
            dve.wait_ge(wvo_copied, 4)
            dve.tensor_copy(wvo_hi[:, :, :], wvo_raw[:, :, :]).then_inc(half_wvo, 1)
            dve.wait_ge(half_wvo, 1)
            dve.tensor_tensor(wvo_lo[:, :, :], wvo_raw[:, :, :], wvo_hi[:, :, :].bitcast(F32),
                              ALU.subtract).then_inc(wvo_split, 1)
            split_g(0)
            dve.memset(carrier[:, :], 0.0).then_inc(y_added, 1)
            dve.wait_ge(x_loaded, 16)

            def neg_max(g, n, slot, i):
                w = (i + 1) * P
                for h in range(2):
                    dve.wait_ge(scores_ready, 8 * g + 2 * n + h + 1)
                    last = dve.tensor_reduce(negmax[:, i, h:h + 1], s_bank[slot][h][:, 0:w], AX.X, ALU.max,
                                             negate=True)
                    if n == 0 or h == 1:
                        last.then_inc(negmax_ready, 1)

            def add_y(g, n, tile0):
                dve.wait_ge(probs_ready, 8 * g + 4 * n + 4)
                two = slice(2 - 2 * n, 4 - 2 * n)
                dve.reciprocal(rsums[:, two, :], sums[:, two, :]).then_inc(rsums_ready, 1)
                dve.wait_ge(rsums_ready, 2 * g + n + 1)
                dve.wait_ge(y_psum, 8 * g + 4 * n + 4)
                for h in range(2):
                    for k in range(2):
                        i = 3 - 2 * n - k
                        at = (k * 2 + h) * C
                        r1 = x_sb[:, tile0 + i, :]
                        if h:
                            dve.wait_ge(y_added, 8 * g + 4 * n + k + 2)
                        dve.scalar_tensor_tensor(out=r1, in0=y_bank[n][:, at:at + C], scalar=rsums[:, i, h:h + 1],
                                                 in1=r1, op0=ALU.mult, op1=ALU.add).then_inc(y_added, 1)

            def step(g, tile0):
                neg_max(g, 0, 0, 3)
                neg_max(g, 1, 1, 2)
                copy_u(g)
                copy_tr(g, 1, 0, pT[:, 0, :], slice(0, S))
                neg_max(g, 2, 0, 1)
                copy_tr(g, 3, 0, pT[:, 2, 0:3 * P], slice(0, 3 * P))
                neg_max(g, 3, 1, 0)
                add_y(g, 0, tile0)
                split_g(g + 1)
                add_y(g, 1, tile0)

            with dve.Fori(0, B) as b:
                with dve.Fori(0, PAIRS) as p:
                    step(b * PAIRS + p, b * NT)
                wait_for(y_added, 8 * PAIRS * (b + 1) + 1, 0)
                for i in range(NT):
                    dve.bn_stats(stats[:, i, :], x_sb[:, b * NT + i, :]).then_inc(stats_ready, 1)
                wait_for(stats_ready, b * NT + NT, 1)
                for i in range(NT):
                    last = dve.bn_aggr(aggr[:, i, :], stats[:, i, :])
                last.then_inc(aggr_ready, 1)
                dve.wait_ge(aggr_ready, b + 1)
                dve.tensor_copy(meanvar[:, bass.ds(b * NT, NT), :], aggr[:, :, :]).then_inc(meanvar_ready, 1)


            def pick_outs(k, picks, dst, mask, outs, done):
                for n in picks:
                    e = SUMMED + n
                    if n == 0:
                        dve.wait_ge(outs, k * PICKED + 1)
                        dve.tensor_tensor(dst[:, :], pick_bank[0][:, :], mask[:, e, :], ALU.mult).then_inc(done, 1)
                    else:
                        wait_for(outs, k * PICKED + n + 1, 4 + n)
                        wait_for(done, k * PICKED + n, 8 + n)
                        dve.copy_predicated(dst[:, :], mask[:, e, :].bitcast(mybir.dt.uint16), pick_bank[n % 3][:, :]
                                            ).then_inc(done, 1)

            def add_summed(k, dst, psum, picked, done):
                dve.wait_ge(picked, (k + 1) * PICKED)
                dve.wait_ge(psum, k + 1)
                dve.tensor_tensor(dst[:, :], dst[:, :], sum_bank[:, :], ALU.add).then_inc(done, 1)

            def choose(k):
                dve.wait_ge(logits_psum, k + 1)
                dve.tensor_tensor(logits[:, :, :], logits_bank[:, 0:NT * E].rearrange("p (t e) -> p t e", e=E),
                                  bg_sb[:, :].unsqueeze(1).broadcast_to([P, NT, E]), ALU.add).then_inc(argmax_step, 1)
                dve.wait_ge(argmax_step, 5 * k + 1)
                dve.tensor_reduce(best[:, :], logits[:, :, :], AX.X, ALU.max).then_inc(argmax_step, 1)
                dve.wait_ge(argmax_step, 5 * k + 2)
                dve.tensor_tensor(ranked[:, :, :], logits[:, :, :], best[:, :].unsqueeze(2).broadcast_to([P, NT, E]),
                                  ALU.is_equal).then_inc(argmax_step, 1)
                dve.wait_ge(argmax_step, 5 * k + 3)
                dve.tensor_tensor(ranked[:, :, :], ranked[:, :, :], rank[:, :].unsqueeze(1).broadcast_to([P, NT, E]),
                                  ALU.mult).then_inc(argmax_step, 1)
                dve.wait_ge(argmax_step, 5 * k + 4)
                dve.tensor_reduce(best[:, :], ranked[:, :, :], AX.X, ALU.max).then_inc(argmax_step, 1)
                dve.wait_ge(argmax_step, 5 * k + 5)
                dve.tensor_tensor(chosen[:, :, :], ranked[:, :, :], best[:, :].unsqueeze(2).broadcast_to([P, NT, E]),
                                  ALU.is_equal).then_inc(chosen_ready, 1)

            def slots(g, parity):
                def pick_h(picks):
                    if live(g):
                        if picks[0] == 0:
                            dve.wait_ge(spread_ready, (g + 1) * E)
                            if not first(g):
                                dve.wait_ge(h_ready, g)
                        pick_outs(g, picks, h_pick, spread[:, parity, :, :], h_outs, h_picked)

                def pick_y(picks):
                    if live(g - 1):
                        if picks[0] == 0 and not first(g - 1):
                            dve.wait_ge(back_psum, g - 1)
                        pick_outs(g - 1, picks, yT_sb, spread[:, 1 - parity, :, :], y_outs, y_picked)

                pick_h((0,))
                pick_h((1,))
                if live(g + 1):
                    choose(g + 1)
                pick_h((2,))
                pick_h((3,))
                if live(g + 1):
                    wait_for(chosenT_psum, g + 2, 4)
                    dve.tensor_copy(chosenT[:, bass.ds(g + 1, 1), :].rearrange("e n s -> e (n s)"),
                                    chosenT_bank[0:E, :]).then_inc(chosenT_ready, 1)
                if live(g - 2):
                    if not first(g - 2):
                        dve.wait_ge(out_ready, g - 2)
                    dve.wait_ge(x1_kept, 16 * (g - 1))
                    dve.wait_ge(back_psum, g - 1)
                    dve.tensor_tensor(r2[:, :, :], back_bank[:, :].rearrange("p (t c) -> p t c", c=C),
                                      x_sb[:, bass.ds((g - 2) * NT, NT), :], ALU.add).then_inc(r2_ready, 1)
                pick_h((4,))
                if live(g):
                    add_summed(g, h_pick, h_psum, h_picked, h_summed)
                if live(g - 2):
                    wait_for(r2_ready, g - 1, 2)
                    for i in range(NT):
                        dve.bn_stats(stats[:, i, :], r2[:, i, :]).then_inc(r2_stats, 1)
                if live(g - 2):
                    wait_for(r2_stats, (g - 1) * NT, 3)
                    for i in range(NT):
                        last = dve.bn_aggr(aggr[:, i, :], stats[:, i, :])
                    last.then_inc(r2_aggr, 1)
                pick_y((0,))
                pick_y((1,))
                if live(g + 2):
                    if not first(g + 2):
                        dve.wait_ge(x1T_psum, g + 2)
                        dve.wait_ge(x1_kept, 16 * (g + 2))
                    for i in range(NT):
                        tile = (g + 2) * NT + i
                        last = dve.tensor_scalar(x1_now[:, i, :], x_sb[:, bass.ds(tile, 1), :].rearrange("p n c -> p (n c)"),
                                                 meanvar[:, bass.ds(tile, 1), 0], rstd1[:, bass.ds(tile, 1)],
                                                 ALU.subtract, ALU.mult)
                    last.then_inc(x1_ready, 1)
                if live(g):
                    dve.wait_ge(h_rounded, g + 1)
                    dve.tensor_tensor(h_lo[:, parity, :], h_32[:, :], h_hi[:, parity, :].bitcast(F32), ALU.subtract
                                      ).then_inc(h_split, 1)
                pick_y((2,))
                pick_y((3,))
                if live(g + 2):
                    dve.wait_ge(x1T_rounded, g + 3)
                    dve.tensor_tensor(x1T_lo[:, parity, :], x1T_bank[:, :], x1T_hi[:, parity, :].bitcast(F32),
                                      ALU.subtract).then_inc(x1T_split, 1)
                pick_y((4,))
                if live(g - 1):
                    add_summed(g - 1, yT_sb, yT_psum, y_picked, yT_summed)

            dve.wait_ge(bg_loaded, 16)
            dve.wait_ge(rstd1_ready, 2)
            expert_slots(dve, slots)


def kernel(**inputs):
    import numpy as _np
    import concourse.bacc as _bacc
    from concourse import mybir as _mybir
    from concourse.bass_utils import run_bass_kernel_spmd as _run

    a = {k[3:]: _np.asarray(v) for k, v in inputs.items()}
    x = a["attn_x"]
    B, S, C = x.shape
    H, D, _ = a["attn_w_q"].shape
    E = a["ffn_W1"].shape[0]
    pairs = H * D // 128
    arrays = {
        "x": x.reshape(B * S, C),
        "xT": x.transpose(0, 2, 1),
        "wq": a["attn_w_q"].reshape(pairs, 128, C),
        "wk": a["attn_w_k"].reshape(pairs, 128, C),
        "wv": a["attn_w_v"].reshape(pairs, 128, C),
        "wo": a["attn_w_o"].reshape(pairs, 128, C),
        "Wg": a["ffn_Wg"],
        "bg": a["ffn_bg"].reshape(1, E),
        "W1": a["ffn_W1"].transpose(1, 0, 2),
        "W2": a["ffn_W2"].transpose(1, 0, 2),
        "b12": _np.concatenate([a["ffn_b1"], a["ffn_b2"]], axis=1),
    }
    arrays = {f"in_{k}": _np.ascontiguousarray(v) for k, v in arrays.items()}
    nc = _bacc.Bacc("TRN2", target_bir_lowering=False, num_devices=1)
    args = [nc.dram_tensor(k, v.shape, _mybir.dt.from_np(v.dtype), kind="ExternalInput").ap() for k, v in arrays.items()]
    out = nc.dram_tensor("out", (B * S, C), _mybir.dt.float32, kind="ExternalOutput").ap()
    layer(nc, *args, out)
    r = _run(nc, [arrays], core_ids=[0])
    return r.results[0]["out"].reshape(B, S, C)
```

```python
from contextlib import ExitStack

import concourse.bass as bass
from concourse import mybir

F32 = mybir.dt.float32
F32R = mybir.dt.float32r
BF16 = mybir.dt.bfloat16
ACT = mybir.ActivationFunctionType
ALU = mybir.AluOpType
AX = mybir.AxisListType

P = 128
MASKED = -1e30
LN_EPS = 1e-5


def layer(nc, x, xT, wq, wk, wv, wo, Wg, bg, W1, W2, b12, out):
    B, C, S = xT.shape
    PAIRS = wq.shape[0]
    E = Wg.shape[1]
    D = P // 2
    NT = S // P
    TILES = B * NT
    STEPS = B * PAIRS
    QSCALE = float(D) ** -0.5
    SUMMED = 3
    PICKED = E - SUMMED
    assert C == P and NT == 4

    with ExitStack() as ctx:
        def sb(name, shape, dt):
            return ctx.enter_context(nc.sbuf_tensor(name, shape, dt))

        def sem(name):
            return ctx.enter_context(nc.semaphore(name))

        x_sb = sb("x_sb", [P, TILES, C], F32)
        meanvar = sb("meanvar", [P, TILES, 2], F32)
        rstd1 = sb("rstd1", [P, TILES], F32)
        ident = sb("ident", [P, P], F32)
        zeros = sb("zeros", [P, E * P], F32)
        carrier = sb("carrier", [P, 16], F32)
        eps = sb("eps", [P, TILES], F32)
        minus_half = sb("minus_half", [P, TILES], F32)
        stats = sb("stats", [P, NT, 6], F32)
        aggr = sb("aggr", [P, NT, 2], F32)
        w1_hi = sb("w1_hi", [P, E, P], F32R)
        w1_lo = sb("w1_lo", [P, E, P], F32R)
        w2_hi = sb("w2_hi", [P, E, P], F32R)
        w2_lo = sb("w2_lo", [P, E, P], F32R)
        w1_raw = sb("w1_raw", [P, E, P], F32)
        w2_raw = sb("w2_raw", [P, E, P], F32)
        wg_raw = sb("wg_raw", [P, E], F32)
        wg_halves = sb("wg_halves", [P, 2, E], F32R)
        bg_sb = sb("bg_sb", [P, E], F32)
        b_raw = sb("b_raw", [E, 2 * P], F32)
        b_halves = sb("b_halves", [E, 2, 2 * P], F32R)
        rank = sb("rank", [P, E], F32)
        pick_raw = sb("pick_raw", [E, E, P], F32)
        pick = sb("pick", [E, E, P], F32R)
        x1_now = sb("x1_now", [P, NT, C], F32)

        attn = ctx.enter_context(ExitStack())

        def sb1(name, shape, dt):
            return attn.enter_context(nc.sbuf_tensor(name, shape, dt))

        xT_32 = sb1("xT_32", [P, B, S], F32)
        xT_hi = sb1("xT_hi", [P, B, S], F32R)
        xT_lo = sb1("xT_lo", [P, B, S], F32R)
        xT_now = sb1("xT_now", [P, 2, S], F32R)
        wqk_halves = sb1("wqk_halves", [P, PAIRS, 2, 2, C], F32R)
        wqk_now = sb1("wqk_now", [P, 2, 2, C], F32R)
        wvo_hi = sb1("wvo_hi", [P, PAIRS, 2 * C], F32R)
        wvo_lo = sb1("wvo_lo", [P, PAIRS, 2 * C], F32R)
        mask = sb1("mask", [P, S], F32)
        g_32 = sb1("g_32", [P, 2, S], F32)
        g_hi = sb1("g_hi", [P, 2, S], F32R)
        g_lo = sb1("g_lo", [P, 2, S], F32R)
        u_sb = sb1("u_sb", [P, NT, 2 * C], F32)
        negmax = sb1("negmax", [P, NT, 2], F32)
        sums = sb1("sums", [P, NT, 2], F32)
        rsums = sb1("rsums", [P, NT, 2], F32)
        with ExitStack() as setup:
            def sb0(name, shape, dt):
                return setup.enter_context(nc.sbuf_tensor(name, shape, dt))

            wq_sb = sb0("wq_sb", [P, PAIRS, C], F32)
            wk_sb = sb0("wk_sb", [P, PAIRS, C], F32)
            wv_sb = sb0("wv_sb", [P, PAIRS, C], F32)
            wo_sb = sb0("wo_sb", [P, PAIRS, C], F32)
        probs = sb1("probs", [P, 2, 2, S], F32)
        pT = sb1("pT", [P, 6, S], F32)

        attn.close()
        x1T_hi = sb("x1T_hi", [P, 2, S], F32R)
        x1T_lo = sb("x1T_lo", [P, 2, S], F32R)
        logits = sb("logits", [P, NT, E], F32)
        best = sb("best", [P, NT], F32)
        ranked = sb("ranked", [P, NT, E], F32)
        chosen = sb("chosen", [P, NT, E], F32)
        chosenT = sb("chosenT", [E, B, S], F32R)
        spread = sb("spread", [P, 2, E, S], BF16)
        m1_hi = sb("m1_hi", [P, SUMMED, S], F32R)
        m1_lo = sb("m1_lo", [P, SUMMED, S], F32R)
        m2_hi = sb("m2_hi", [P, SUMMED, S], F32R)
        m2_lo = sb("m2_lo", [P, SUMMED, S], F32R)
        h_pick = sb("h_pick", [P, S], F32)
        h_32 = sb("h_32", [P, S], F32)
        h_hi = sb("h_hi", [P, 2, S], F32R)
        h_lo = sb("h_lo", [P, 2, S], F32R)
        yT_sb = sb("yT_sb", [P, S], F32)
        r2 = sb("r2", [P, NT, C], F32)
        rstd2 = sb("rstd2", [P, NT], F32)
        shift2 = sb("shift2", [P, NT], F32)
        out_sb = sb("out_sb", [P, NT, C], F32)

        bank = [ctx.enter_context(nc.psum_tensor(f"bank{i}", [P, S], F32)) for i in range(8)]
        s_bank = [[bank[0], bank[1]], [bank[2], bank[3]]]
        t_bank = [bank[4], bank[5]]
        y_bank = [bank[6], bank[7]]


        def product_bank(done, n, h):
            return bank[(4 if done is wqk_psum else 2) + 2 * n + h]

        def wqk_hi_of(m, h):
            return wqk_halves[:, m:m + 4, 0, h, :]

        def wqk_lo_of(m, h):
            return wqk_halves[:, m:m + 4, 1, h, :]

        def wvo_hi_of(m, h):
            return wvo_hi[:, m:m + 4, h * C:(h + 1) * C]

        def wvo_lo_of(m, h):
            return wvo_lo[:, m:m + 4, h * C:(h + 1) * C]

        x1T_bank = back_bank = bank[0]
        logits_bank = chosenT_bank = bank[1]
        spread_bank = [bank[2], bank[3]]
        sum_bank = bank[4]
        pick_bank = [bank[5], bank[6], bank[7]]

        def live(g):
            return not isinstance(g, int) or 0 <= g < B

        def first(g):
            return isinstance(g, int) and g == 0

        def expert_slots(engine, slots):
            for g in range(-2, 2):
                slots(g, g % 2)
            with engine.Fori(1, B // 2 - 1) as half:
                for parity in range(2):
                    slots(half * 2 + parity, parity)
            for g in range(B - 2, B + 2):
                slots(g, g % 2)

        x_loaded = sem("x_loaded")
        wqk_first_loaded = sem("wqk_first_loaded")
        wqk_rest_loaded = sem("wqk_rest_loaded")
        wvo_loaded = sem("wvo_loaded")
        xT_first_loaded = sem("xT_first_loaded")
        xT_rest_loaded = sem("xT_rest_loaded")
        wqk_moved = sem("wqk_moved")
        pool_zero = sem("pool_zero")
        consts_ready = sem("consts_ready")
        xT_split = sem("xT_split")
        xT_moved = sem("xT_moved")
        wqk_psum = sem("wqk_psum")
        wqk_rounded = sem("wqk_rounded")
        wqk_split = sem("wqk_split")
        wvo_split = sem("wvo_split")
        half_xT = sem("half_xT")
        g_psum = sem("g_psum")
        u_psum = sem("u_psum")
        g_rounded = sem("g_rounded")
        u_copied_act = sem("u_copied_act")
        u_copied_dve = sem("u_copied_dve")
        wvo_psum = sem("wvo_psum")
        wvo_rounded = sem("wvo_rounded")
        g_split = sem("g_split")
        g_joined = sem("g_joined")
        scores_ready = sem("scores_ready")
        negmax_ready = sem("negmax_ready")
        probs_ready = sem("probs_ready")
        tr_psum = sem("tr_psum")
        tr_dve = sem("tr_dve")
        tr_act = sem("tr_act")
        y_psum = sem("y_psum")
        rsums_ready = sem("rsums_ready")
        y_added = sem("y_added")
        stats_ready = sem("stats_ready")
        aggr_ready = sem("aggr_ready")
        meanvar_ready = sem("meanvar_ready")
        w_loaded = sem("w_loaded")
        bg_loaded = sem("bg_loaded")
        w_rounded = sem("w_rounded")
        w_split = sem("w_split")
        small_raw = sem("small_raw")
        small_rounded = sem("small_rounded")
        var1_ready = sem("var1_ready")
        var2_ready = sem("var2_ready")
        pow2_ready = sem("pow2_ready")
        rstd1_ready = sem("rstd1_ready")
        x1_ready = sem("x1_ready")
        x1_kept = sem("x1_kept")
        x1T_psum = sem("x1T_psum")
        x1T_rounded = sem("x1T_rounded")
        x1T_split = sem("x1T_split")
        logits_psum = sem("logits_psum")
        argmax_step = sem("argmax_step")
        chosen_ready = sem("chosen_ready")
        chosenT_psum = sem("chosenT_psum")
        chosenT_ready = sem("chosenT_ready")
        spread_psum = sem("spread_psum")
        spread_ready = sem("spread_ready")
        m1_ready = sem("m1_ready")
        h_outs = sem("h_outs")
        h_picked = sem("h_picked")
        h_psum = sem("h_psum")
        h_summed = sem("h_summed")
        h_ready = sem("h_ready")
        h_rounded = sem("h_rounded")
        h_split = sem("h_split")
        m2_ready = sem("m2_ready")
        y_outs = sem("y_outs")
        y_picked = sem("y_picked")
        yT_psum = sem("yT_psum")
        yT_summed = sem("yT_summed")
        back_psum = sem("back_psum")
        r2_ready = sem("r2_ready")
        r2_stats = sem("r2_stats")
        r2_aggr = sem("r2_aggr")
        rstd2_ready = sem("rstd2_ready")
        out_ready = sem("out_ready")
        stored = sem("stored")

        block = ctx.enter_context(nc.Block())

        @block.sync
        def _(sp):
            half = slice(0, PAIRS // 2)
            rest = slice(PAIRS // 2, PAIRS)
            for sb_tile, dram in ((wq_sb, wq), (wk_sb, wk)):
                sp.dma_start(sb_tile[:, half, :], dram[half].rearrange("a p c -> p a c")).then_inc(wqk_first_loaded, 16)
            sp.dma_start(xT_32[:, 0, :], xT[0]).then_inc(xT_first_loaded, 16)
            for sb_tile, dram in ((wq_sb, wq), (wk_sb, wk)):
                sp.dma_start(sb_tile[:, rest, :], dram[rest].rearrange("a p c -> p a c")).then_inc(wqk_rest_loaded, 16)
            for sb_tile, dram in ((wv_sb, wv), (wo_sb, wo)):
                sp.dma_start(sb_tile[:, :, :], dram.rearrange("a p c -> p a c")).then_inc(wvo_loaded, 16)
            sp.dma_start(xT_32[:, 1:B, :], xT[1:B].rearrange("b c s -> c b s")).then_inc(xT_rest_loaded, 16)

            def move_wqk(pair):
                sp.dma_start(wqk_now[:, :, :, :].rearrange("p a h c -> p (a h c)").bitcast(F32),
                             wqk_halves[:, bass.ds(pair, 1), :, :, :].rearrange("p n a h c -> p (n a h c)").bitcast(F32)
                             ).then_inc(wqk_moved, 16)

            def next_wqk(n, pair):
                sp.wait_ge(g_psum, 2 * n)
                move_wqk(pair)

            def move_xT(b):
                for half, src in enumerate((xT_hi, xT_lo)):
                    sp.dma_start(xT_now[:, half, :].bitcast(F32),
                                 src[:, bass.ds(b, 1), :].rearrange("p n s -> p (n s)").bitcast(F32)
                                 ).then_inc(xT_moved, 16)

            sp.wait_ge(wqk_split, 2)
            move_wqk(0)
            sp.wait_ge(xT_split, 1)
            move_xT(0)
            sp.dma_start(x_sb[:, :, :], x.rearrange("(t p) c -> p t c", p=P)).then_inc(x_loaded, 16)
            sp.dma_start(w1_raw[:, :, :], W1).then_inc(w_loaded, 16)
            sp.dma_start(w2_raw[:, :, :], W2).then_inc(w_loaded, 16)
            sp.dma_start(wg_raw[:, :], Wg).then_inc(w_loaded, 16)
            sp.dma_start(bg_sb[:, :], bg.broadcast_to([P, E])).then_inc(bg_loaded, 16)
            sp.dma_start(b_raw[:, :], b12).then_inc(w_loaded, 16)
            sp.wait_ge(wqk_split, 4)
            with sp.Fori(0, B - 1) as b:
                with sp.Fori(0, PAIRS - 1) as p:
                    next_wqk(b * PAIRS + p + 1, p + 1)
                next_wqk(b * PAIRS + PAIRS, 0)
                sp.wait_ge(xT_split, B)
                sp.wait_ge(u_psum, b * PAIRS + PAIRS)
                move_xT(b + 1)
            with sp.Fori(0, PAIRS - 1) as p:
                next_wqk((B - 1) * PAIRS + p + 1, p + 1)
            next_wqk(B * PAIRS, 0)

            def keep_x1(g):
                sp.wait_ge(x1_ready, g + 1)
                sp.dma_start(x_sb[:, bass.ds(g * NT, NT), :], x1_now[:, :, :]).then_inc(x1_kept, 16)

            def store(g):
                sp.wait_ge(out_ready, g + 1)
                sp.dma_start(out_groups[bass.ds(g, 1)].rearrange("n p t c -> (n p) t c"), out_sb[:, :, :]
                             ).then_inc(stored, 16)

            out_groups = out.rearrange("(g t p) c -> g p t c", p=P, t=NT)
            for g in range(4):
                keep_x1(g)
            with sp.Fori(4, B) as g:
                keep_x1(g)
                store(g - 4)
            for g in range(B - 4, B):
                store(g)
            sp.wait_ge(stored, 16 * B)

        @block.gpsimd
        def _(pool):
            pool.memset(ident[:, :], 0.0).then_inc(pool_zero, 1)
            pool.memset(mask[:, :], 0.0).then_inc(pool_zero, 1)
            pool.memset(zeros[:, :], 0.0).then_inc(pool_zero, 1)
            pool.wait_ge(pool_zero, 3)
            pool.affine_select(out=ident[:, :], in_=ident[:, :], compare_op=ALU.not_equal, fill=1.0, base=0,
                               pattern=[[-1, P]], channel_multiplier=1).then_inc(consts_ready, 1)
            pool.affine_select(out=mask[:, S - P:S], in_=mask[:, S - P:S], compare_op=ALU.is_ge, fill=MASKED, base=0,
                               pattern=[[-1, P]], channel_multiplier=1).then_inc(consts_ready, 1)

            def split_xT(batches):
                for b in batches:
                    pool.tensor_tensor(xT_hi[:, b, :], xT_32[:, b, :], zeros[:, 0:S], ALU.add).then_inc(half_xT, 1)
                for b in batches:
                    pool.wait_ge(half_xT, b + 1)
                    pool.tensor_tensor(xT_lo[:, b, :], xT_32[:, b, :], xT_hi[:, b, :].bitcast(F32), ALU.subtract
                                       ).then_inc(xT_split, 1)

            pool.wait_ge(xT_first_loaded, 16)
            split_xT(range(1))

            def join_g(n):
                pool.wait_ge(g_split, 2 * n + 2)
                pool.tensor_tensor(g_32[:, :, :], g_hi[:, :, :].bitcast(F32), g_lo[:, :, :].bitcast(F32), ALU.add
                                   ).then_inc(g_joined, 1)

            join_g(0)
            pool.wait_ge(xT_rest_loaded, 16)
            split_xT(range(1, B))

            def joins(b):
                with pool.Fori(0, PAIRS) as p:
                    join_g(b * PAIRS + p + 1)

            def first_rstd(tiles, batches):
                pool.wait_ge(meanvar_ready, batches)
                n = tiles.stop - tiles.start
                pool.tensor_tensor(rstd1[:, tiles], meanvar[:, tiles, 1], eps[:, 0:n], ALU.add).then_inc(var1_ready, 1)
                pool.wait_ge(var1_ready, batches - B + 2)
                pool.tensor_tensor(rstd1[:, tiles], rstd1[:, tiles], minus_half[:, 0:n], ALU.pow
                                   ).then_inc(rstd1_ready, 1)

            joins(0)
            for e in range(E):
                pool.memset(rank[:, e:e + 1], float(E - e)).then_inc(small_raw, 1)
            pool.memset(pick_raw[:, :, :], 0.0).then_inc(small_raw, 1)
            pool.memset(eps[:, :], LN_EPS).then_inc(small_raw, 1)
            pool.memset(minus_half[:, :], -0.5).then_inc(small_raw, 1)
            pool.wait_ge(small_raw, E + 3)
            pool.affine_select(out=pick_raw[:, :, :], in_=pick_raw[:, :, :], compare_op=ALU.not_equal, fill=1.0,
                               base=0, pattern=[[-1, E], [0, P]], channel_multiplier=1).then_inc(small_raw, 1)
            pool.wait_ge(small_raw, E + 4)
            pool.tensor_tensor(pick[:, :, :].rearrange("k e p -> k (e p)"),
                               pick_raw[:, :, :].rearrange("k e p -> k (e p)"), zeros[0:E, :], ALU.add
                               ).then_inc(small_rounded, 1)
            pool.wait_ge(w_loaded, 64)
            flat = [t[:, :, :].rearrange("p e i -> p (e i)") for t in (w1_raw, w1_hi, w1_lo, w2_raw, w2_hi, w2_lo)]
            parts = (flat[0:3], flat[3:6], (wg_raw[:, :], wg_halves[:, 0, :], wg_halves[:, 1, :]),
                     (b_raw[:, :], b_halves[:, 0, :], b_halves[:, 1, :]))
            for raw, hi, lo in parts:
                pool.tensor_tensor(hi, raw, zeros[0:raw.shape[0], 0:raw.shape[1]], ALU.add).then_inc(w_rounded, 1)
            pool.wait_ge(w_rounded, 4)
            for raw, hi, lo in parts:
                pool.tensor_tensor(lo, raw, hi.bitcast(F32), ALU.subtract).then_inc(w_split, 1)
            with pool.Fori(1, B - 1) as b:
                joins(b)
            first_rstd(slice(0, TILES - NT), B - 1)
            joins(B - 1)
            first_rstd(slice(TILES - NT, TILES), B)

            def products(src, dst, mask, done, spread_at=None):
                for e in range(SUMMED):
                    if spread_at is not None:
                        pool.wait_ge(spread_ready, spread_at + e + 1)
                    for half in range(2):
                        pool.tensor_tensor(dst[half][:, e, :], src[half], mask[:, e, :], ALU.mult).then_inc(done, 1)

            def slots(g, parity):
                if live(g - 2):
                    pool.wait_ge(r2_aggr, g - 1)
                    pool.tensor_tensor(rstd2[:, :], aggr[:, :, 1], eps[:, 0:NT], ALU.add).then_inc(var2_ready, 1)
                    pool.tensor_tensor(shift2[:, :], zeros[:, 0:NT], aggr[:, :, 0], ALU.subtract).then_inc(var2_ready, 1)
                    pool.wait_ge(var2_ready, 2 * (g - 1))
                    pool.tensor_tensor(rstd2[:, :], rstd2[:, :], minus_half[:, 0:NT], ALU.pow).then_inc(pow2_ready, 1)
                    pool.wait_ge(pow2_ready, g - 1)
                    pool.tensor_tensor(shift2[:, :], shift2[:, :], rstd2[:, :], ALU.mult).then_inc(rstd2_ready, 1)
                if live(g + 1):
                    pool.wait_ge(x1T_split, g + 2)
                    if not first(g + 1):
                        pool.wait_ge(h_psum, g + 1)
                    products((x1T_hi[:, 1 - parity, :].bitcast(F32), x1T_lo[:, 1 - parity, :].bitcast(F32)),
                             (m1_hi, m1_lo), spread[:, 1 - parity, :, :], m1_ready, (g + 1) * E)
                if live(g):
                    pool.wait_ge(h_split, g + 1)
                    if not first(g):
                        pool.wait_ge(yT_psum, g)
                    products((h_hi[:, parity, :].bitcast(F32), h_lo[:, parity, :].bitcast(F32)), (m2_hi, m2_lo),
                             spread[:, parity, :, :], m2_ready)

            expert_slots(pool, slots)

        @block.tensor
        def _(pe):
            def three(out_ap, a_hi, a_lo, b_hi, b_lo, **last):
                pe.matmul(out_ap, a_lo, b_hi, start=True, stop=False)
                pe.matmul(out_ap, a_hi, b_lo, start=False, stop=False)
                return pe.matmul(out_ap, a_hi, b_hi, start=False, stop=True)

            def batch_of(t, b, w=slice(0, S)):
                return t[:, bass.ds(b, 1), w].rearrange("p n s -> p (n s)")

            def project_g(n, b):
                pe.wait_ge(wqk_moved, 16 * (n + 1))
                for h in range(2):
                    three(s_bank[0][h][:, :], wqk_now[:, 0, h, :], wqk_now[:, 1, h, :], batch_of(xT_hi, b),
                          batch_of(xT_lo, b)).then_inc(g_psum, 1)

            def project_u(pair, b):
                pe.wait_ge(xT_moved, 32 * b + 32)
                for j in range(NT):
                    t = slice(j * P, (j + 1) * P)
                    c = slice(j % 2 * 2 * C, (j % 2 + 1) * 2 * C)
                    last = three(y_bank[j // 2][:, c], xT_now[:, 0, t], xT_now[:, 1, t], wvo_hi[:, pair, :],
                                 wvo_lo[:, pair, :])
                last.then_inc(u_psum, 1)

            def scores(slot, i, b, g=None):
                w = (i + 1) * P
                t = slice(i * P, w)
                parts = ((g_lo, xT_hi), (g_hi, xT_lo), (g_hi, xT_hi)) if i else ((g_32, xT_32),)
                for h in range(2):
                    if g is not None:
                        pe.wait_ge(g_split, 2 * g + h + 1)
                    for n, (a, c) in enumerate(parts):
                        last = pe.matmul(s_bank[slot][h][:, 0:w], a[:, h, t], batch_of(c, b, slice(0, w)),
                                         start=(n == 0), stop=(n == len(parts) - 1))
                    last.then_inc(scores_ready, 1)

            def transposes(use, slot, blocks):
                for n, (h, j) in enumerate(blocks):
                    last = pe.transpose(t_bank[use % 2][:, n * P:(n + 1) * P], probs[:, slot, h, j * P:(j + 1) * P],
                                        ident[:, :])
                last.then_inc(tr_psum, 1)

            def pu(use, i, h, first=0):
                at = ((3 - i) % 2 * 2 + h) * C
                for j in range(i + 1):
                    last = pe.matmul(y_bank[(3 - i) // 2][:, at:at + C],
                                     pT[:, use, (first + j) * P:(first + j + 1) * P],
                                     u_sb[:, j, h * C:(h + 1) * C], start=(j == 0), stop=(j == i))
                last.then_inc(y_psum, 1)

            def step(g, p, b, b_next):
                scores(0, 3, b, g)
                scores(1, 2, b)
                pe.wait_ge(y_added, 8 * g + 1)
                project_u(p, b)
                pe.wait_ge(probs_ready, 8 * g + 1)
                transposes(0, 0, [(0, j) for j in range(4)])
                pe.wait_ge(probs_ready, 8 * g + 2)
                transposes(1, 0, [(1, j) for j in range(4)])
                scores(0, 1, b)
                pe.wait_ge(u_copied_act, g + 1)
                pe.wait_ge(u_copied_dve, g + 1)
                pe.wait_ge(tr_dve, 2 * g + 1)
                pu(0, 3, 0)
                pe.wait_ge(tr_act, 4 * g + 1)
                pu(1, 3, 1)
                pe.wait_ge(probs_ready, 8 * g + 3)
                transposes(2, 1, [(0, j) for j in range(3)])
                pe.wait_ge(probs_ready, 8 * g + 4)
                transposes(3, 1, [(1, j) for j in range(3)])
                pe.wait_ge(g_joined, g + 1)
                scores(1, 0, b)
                pe.wait_ge(probs_ready, 8 * g + 6)
                pe.wait_ge(tr_dve, 2 * g + 2)
                transposes(4, 0, [(h, j) for h in range(2) for j in range(2)])
                pu(2, 2, 0)
                pe.wait_ge(tr_act, 4 * g + 2)
                pu(3, 2, 1)
                pe.wait_ge(probs_ready, 8 * g + 8)
                transposes(5, 1, [(0, 0), (1, 0)])
                project_g(g + 1, b_next)
                pe.wait_ge(tr_act, 4 * g + 3)
                pu(4, 1, 0)
                pu(4, 1, 1, first=2)
                pe.wait_ge(tr_act, 4 * g + 4)
                pu(5, 0, 0)
                pu(5, 0, 1, first=1)

            def weight_products(a, c, n, done):
                for h in range(2):
                    r = slice(h * D, (h + 1) * D)
                    for m in range(4):
                        last = pe.matmul(product_bank(done, n, h)[:, m * C:(m + 1) * C], a[r, n * 4 + m, :],
                                         c[r, n * 4 + m, :], start=True, stop=True)
                    last.then_inc(done, 1)

            pe.wait_ge(wqk_first_loaded, 32)
            weight_products(wq_sb, wk_sb, 0, wqk_psum)
            pe.wait_ge(wqk_rest_loaded, 32)
            weight_products(wq_sb, wk_sb, 1, wqk_psum)
            pe.wait_ge(wvo_loaded, 32)
            weight_products(wv_sb, wo_sb, 0, wvo_psum)
            pe.wait_ge(xT_split, 1)
            project_g(0, 0)
            pe.wait_ge(wqk_split, 2)
            weight_products(wv_sb, wo_sb, 1, wvo_psum)
            pe.wait_ge(consts_ready, 2)
            pe.wait_ge(wvo_split, 4)
            with pe.Fori(0, B - 1) as b:
                with pe.Fori(0, PAIRS - 1) as p:
                    step(b * PAIRS + p, p, b, b)
                pe.wait_ge(xT_split, B)
                step(b * PAIRS + PAIRS - 1, PAIRS - 1, b, b + 1)
            with pe.Fori(0, PAIRS) as p:
                step((B - 1) * PAIRS + p, p, B - 1, B - 1)

            def slots(g, parity):
                def chosen_of(k):
                    return chosenT[:, bass.ds(k, 1), :].rearrange("e n s -> e (n s)")

                def expert(out_bank, w, e, m, **when):
                    (w_hi, w_lo), (m_hi, m_lo) = w, m
                    pe.matmul(out_bank[:, :], w_hi[:, e, :], m_lo, start=when["start"], stop=False)
                    pe.matmul(out_bank[:, :], w_lo[:, e, :], m_hi, start=False, stop=False)
                    return pe.matmul(out_bank[:, :], w_hi[:, e, :], m_hi, start=False, stop=when["stop"])

                def bias(half_of, k):
                    pe.matmul(sum_bank[:, :], b_halves[:, 1, half_of], chosen_of(k), start=False, stop=False)
                    return pe.matmul(sum_bank[:, :], b_halves[:, 0, half_of], chosen_of(k), start=False, stop=True)

                def first_layer(picks):
                    for n in picks:
                        if n >= 3:
                            pe.wait_ge(h_picked, g * PICKED + n - 2)
                        elif not first(g) and not first(g - 1) and n == 0:
                            pe.wait_ge(y_picked, (g - 1) * PICKED)
                        expert(pick_bank[n % 3], (w1_hi, w1_lo), SUMMED + n,
                               (x1T_hi[:, parity, :], x1T_lo[:, parity, :]), start=True, stop=True).then_inc(h_outs, 1)

                def spread_choice(e):
                    pe.matmul(spread_bank[e % 2][:, :], pick[:, e, :], chosen_of(g + 1), start=True, stop=True
                              ).then_inc(spread_psum, 1)

                if live(g):
                    first_layer((0, 1, 2))
                if live(g + 1):
                    pe.wait_ge(x1T_split, g + 2)
                    for i in range(NT):
                        t = slice(i * P, (i + 1) * P)
                        last = three(logits_bank[:, i * E:(i + 1) * E], x1T_hi[:, 1 - parity, t],
                                     x1T_lo[:, 1 - parity, t], wg_halves[:, 0, :], wg_halves[:, 1, :])
                    last.then_inc(logits_psum, 1)
                if live(g):
                    first_layer((3,))
                if live(g - 2):
                    pe.wait_ge(yT_summed, g - 1)
                    for i in range(NT):
                        t = slice(i * P, (i + 1) * P)
                        last = pe.transpose(back_bank[:, t], yT_sb[:, t], ident[:, :])
                    last.then_inc(back_psum, 1)
                if live(g):
                    first_layer((4,))
                if live(g + 1):
                    pe.wait_ge(chosen_ready, g + 2)
                    for i in range(NT):
                        last = pe.transpose(chosenT_bank[0:E, i * P:(i + 1) * P], chosen[:, i, :], ident[:, :])
                    last.then_inc(chosenT_psum, 1)
                if live(g):
                    if not first(g) and not first(g - 1):
                        pe.wait_ge(yT_summed, g - 1)
                    for e in range(SUMMED):
                        pe.wait_ge(m1_ready, (g * SUMMED + e + 1) * 2)
                        expert(sum_bank, (w1_hi, w1_lo), e, (m1_hi[:, e, :], m1_lo[:, e, :]),
                               start=(e == 0), stop=False)
                    bias(slice(0, P), g).then_inc(h_psum, 1)

                for n in range(E):
                    if live(g + 2) and n == 6:
                        pe.wait_ge(x1_ready, g + 3)
                        for i in range(NT):
                            last = pe.transpose(x1T_bank[:, i * P:(i + 1) * P], x1_now[:, i, :], ident[:, :])
                        last.then_inc(x1T_psum, 1)
                    if live(g + 1):
                        if n == 0:
                            pe.wait_ge(chosenT_ready, g + 2)
                        if n >= 2 or not first(g + 1):
                            pe.wait_ge(spread_ready, (g + 1) * E + n - 1)
                    if live(g - 1) and n < PICKED:
                        if n >= 3:
                            pe.wait_ge(y_picked, (g - 1) * PICKED + n - 2)
                        elif live(g) and n == 0:
                            pe.wait_ge(h_picked, (g + 1) * PICKED)
                        expert(pick_bank[n % 3], (w2_hi, w2_lo), SUMMED + n,
                               (h_hi[:, 1 - parity, :], h_lo[:, 1 - parity, :]), start=True, stop=True
                               ).then_inc(y_outs, 1)
                    elif live(g - 1):
                        e = n - PICKED
                        if live(g) and e == 0:
                            pe.wait_ge(h_summed, g + 1)
                        pe.wait_ge(m2_ready, ((g - 1) * SUMMED + e + 1) * 2)
                        expert(sum_bank, (w2_hi, w2_lo), e, (m2_hi[:, e, :], m2_lo[:, e, :]),
                               start=(e == 0), stop=False)
                    if live(g + 1):
                        spread_choice(n)
                if live(g - 1):
                    bias(slice(P, 2 * P), g - 1).then_inc(yT_psum, 1)

            pe.wait_ge(w_split, 4)
            pe.wait_ge(small_rounded, 1)
            expert_slots(pe, slots)

        @block.scalar
        def _(act):
            def round_g(n):
                for h in range(2):
                    act.wait_ge(g_psum, 2 * n + h + 1)
                    act.activation(g_hi[:, h, :], s_bank[0][h][:, :], ACT.Copy).then_inc(g_rounded, 1)

            def copy_u(n):
                act.wait_ge(u_psum, n + 1)
                act.activation(u_sb[:, 0:2, :].rearrange("p a c -> p (a c)"), y_bank[0][:, :], ACT.Copy
                               ).then_inc(u_copied_act, 1)

            def exps(g, n, slot, i, h):
                w = (i + 1) * P
                act.wait_ge(negmax_ready, 8 * g + n)
                act.activation(probs[:, slot, h, 0:w], s_bank[slot][h][:, 0:w], ACT.Exp, scale=-1.0,
                               bias=negmax[:, i, h:h + 1], accum_out=sums[:, i, h:h + 1]).then_inc(probs_ready, 1)

            def copy_tr(g, count, bank_no, dst, w):
                act.wait_ge(tr_psum, 6 * g + count)
                act.activation(dst, t_bank[bank_no][:, w], ACT.Copy).then_inc(tr_act, 1)

            def round_products(n, psum, hi, done):
                for h in range(2):
                    act.wait_ge(psum, 2 * n + h + 1)
                    act.activation(hi(n * 4, h), product_bank(psum, n, h)[:, :].rearrange("p (a c) -> p a c", c=C),
                                   ACT.Copy, scale=QSCALE if psum is wqk_psum else 1.0).then_inc(done, 1)

            round_products(0, wqk_psum, wqk_hi_of, wqk_rounded)
            round_products(1, wqk_psum, wqk_hi_of, wqk_rounded)
            round_products(0, wvo_psum, wvo_hi_of, wvo_rounded)
            round_g(0)
            round_products(1, wvo_psum, wvo_hi_of, wvo_rounded)
            with act.Fori(0, STEPS) as g:
                exps(g, 1, 0, 3, 0)
                exps(g, 2, 0, 3, 1)
                exps(g, 3, 1, 2, 0)
                copy_u(g)
                copy_tr(g, 2, 1, pT[:, 1, :], slice(0, S))
                exps(g, 4, 1, 2, 1)
                exps(g, 5, 0, 1, 0)
                exps(g, 6, 0, 1, 1)
                copy_tr(g, 4, 1, pT[:, 3, 0:3 * P], slice(0, 3 * P))
                exps(g, 7, 1, 0, 0)
                exps(g, 8, 1, 0, 1)
                copy_tr(g, 5, 0, pT[:, 4, :], slice(0, S))
                copy_tr(g, 6, 1, pT[:, 5, 0:2 * P], slice(0, 2 * P))
                round_g(g + 1)

            def slots(g, parity):
                for e in range(E):
                    if live(g) and e == 3:
                        act.wait_ge(h_summed, g + 1)
                        if not first(g):
                            act.wait_ge(h_split, g)
                        act.activation(h_32[:, :], h_pick[:, :], ACT.Gelu).then_inc(h_ready, 1)
                    if live(g) and e == 4:
                        act.wait_ge(h_ready, g + 1)
                        if not first(g) and not first(g - 1):
                            act.wait_ge(yT_psum, g - 1)
                        act.activation(h_hi[:, parity, :], h_32[:, :], ACT.Copy).then_inc(h_rounded, 1)
                    if live(g + 2) and e == 6:
                        act.wait_ge(x1T_psum, g + 3)
                        if live(g):
                            act.wait_ge(m1_ready, (g + 1) * SUMMED * 2)
                            act.wait_ge(h_psum, g + 1)
                        act.activation(x1T_hi[:, parity, :], x1T_bank[:, :], ACT.Copy).then_inc(x1T_rounded, 1)
                    if live(g + 1):
                        act.wait_ge(spread_psum, (g + 1) * E + e + 1)
                        if live(g - 1):
                            if e == 0:
                                act.wait_ge(m2_ready, g * SUMMED * 2)
                            if e >= SUMMED:
                                act.wait_ge(y_picked, (g - 1) * PICKED + e - SUMMED + 1)
                        act.activation(spread[:, 1 - parity, e, :], spread_bank[e % 2][:, :], ACT.Copy
                                       ).then_inc(spread_ready, 1)
                if live(g - 2):
                    act.wait_ge(rstd2_ready, g - 1)
                    if not first(g - 2):
                        act.wait_ge(stored, 16 * (g - 2))
                    for i in range(NT):
                        last = act.activation(out_sb[:, i, :], r2[:, i, :], ACT.Identity, bias=shift2[:, i:i + 1],
                                              scale=rstd2[:, i:i + 1])
                    last.then_inc(out_ready, 1)

            expert_slots(act, slots)

        @block.vector
        def _(dve):
            def split_g(n):
                for h in range(2):
                    dve.wait_ge(g_rounded, 2 * n + h + 1)
                    dve.tensor_tensor(g_lo[:, h, :], s_bank[0][h][:, :], g_hi[:, h, :].bitcast(F32), ALU.subtract
                                      ).then_inc(g_split, 1)

            def copy_u(n):
                dve.wait_ge(u_psum, n + 1)
                dve.tensor_copy(u_sb[:, 2:4, :].rearrange("p a c -> p (a c)"), y_bank[1][:, :]
                                ).then_inc(u_copied_dve, 1)

            def copy_tr(g, count, bank_no, dst, w):
                dve.wait_ge(tr_psum, 6 * g + count)
                dve.tensor_copy(dst, t_bank[bank_no][:, w]).then_inc(tr_dve, 1)

            def wait_for(signal, count, cell):
                dve.wait_ge(signal, count)
                dve.memset(carrier[:, cell:cell + 1], 0.0)

            def split_products(n, psum, rounded, hi, lo, done):
                for h in range(2):
                    dve.wait_ge(rounded, 2 * n + h + 1)
                    dve.scalar_tensor_tensor(out=lo(n * 4, h),
                                             in0=product_bank(psum, n, h)[:, :].rearrange("p (a c) -> p a c", c=C),
                                             scalar=QSCALE if psum is wqk_psum else 1.0, in1=hi(n * 4, h).bitcast(F32),
                                             op0=ALU.mult, op1=ALU.subtract).then_inc(done, 1)

            split_products(0, wqk_psum, wqk_rounded, wqk_hi_of, wqk_lo_of, wqk_split)
            split_products(1, wqk_psum, wqk_rounded, wqk_hi_of, wqk_lo_of, wqk_split)
            split_products(0, wvo_psum, wvo_rounded, wvo_hi_of, wvo_lo_of, wvo_split)
            split_g(0)
            split_products(1, wvo_psum, wvo_rounded, wvo_hi_of, wvo_lo_of, wvo_split)
            dve.memset(carrier[:, 0:1], 0.0).then_inc(y_added, 1)
            dve.wait_ge(x_loaded, 16)

            def mask_scores(g, n, slot, i, heads=(0, 1)):
                w = (i + 1) * P
                for h in heads:
                    s = s_bank[slot][h][:, 0:w]
                    wait_for(scores_ready, 8 * g + 2 * n + h + 1, 5 + 2 * n + h)
                    dve.tensor_tensor_reduce(out=s, in0=s, in1=mask[:, S - w:S], scale=-1.0, scalar=-MASKED,
                                             op0=ALU.add, op1=ALU.min, accum_out=negmax[:, i, h:h + 1]
                                             ).then_inc(negmax_ready, 1)

            def add_y(g, n, tile0):
                dve.wait_ge(probs_ready, 8 * g + 4 * n + 4)
                two = slice(2 - 2 * n, 4 - 2 * n)
                dve.reciprocal(rsums[:, two, :], sums[:, two, :]).then_inc(rsums_ready, 1)
                dve.wait_ge(rsums_ready, 2 * g + n + 1)
                dve.wait_ge(y_psum, 8 * g + 4 * n + 4)
                for h in range(2):
                    for k in range(2):
                        i = 3 - 2 * n - k
                        at = (k * 2 + h) * C
                        r1 = x_sb[:, tile0 + i, :]
                        if h:
                            dve.wait_ge(y_added, 8 * g + 4 * n + k + 2)
                        dve.scalar_tensor_tensor(out=r1, in0=y_bank[n][:, at:at + C], scalar=rsums[:, i, h:h + 1],
                                                 in1=r1, op0=ALU.mult, op1=ALU.add).then_inc(y_added, 1)

            def first_stats(b):
                wait_for(y_added, 8 * PAIRS * (b + 1) + 1, 0)
                for i in range(NT):
                    dve.bn_stats(stats[:, i, :], x_sb[:, b * NT + i, :]).then_inc(stats_ready, 1)
                wait_for(stats_ready, b * NT + NT, 1)
                for i in range(NT):
                    last = dve.bn_aggr(aggr[:, i, :], stats[:, i, :])
                last.then_inc(aggr_ready, 1)
                dve.wait_ge(aggr_ready, b + 1)
                dve.tensor_copy(meanvar[:, bass.ds(b * NT, NT), :], aggr[:, :, :]).then_inc(meanvar_ready, 1)

            def step(g, tile0, stats_of=None):
                mask_scores(g, 0, 0, 3)
                mask_scores(g, 1, 1, 2, (0,))
                copy_u(g)
                copy_tr(g, 1, 0, pT[:, 0, :], slice(0, S))
                mask_scores(g, 1, 1, 2, (1,))
                mask_scores(g, 2, 0, 1)
                if stats_of is not None:
                    first_stats(stats_of)
                copy_tr(g, 3, 0, pT[:, 2, 0:3 * P], slice(0, 3 * P))
                mask_scores(g, 3, 1, 0)
                add_y(g, 0, tile0)
                split_g(g + 1)
                add_y(g, 1, tile0)

            step(0, 0)
            with dve.Fori(1, PAIRS) as p:
                step(p, 0)
            with dve.Fori(1, B) as b:
                step(b * PAIRS, b * NT, stats_of=b - 1)
                with dve.Fori(1, PAIRS) as p:
                    step(b * PAIRS + p, b * NT)
            def pick_outs(k, picks, dst, mask, outs, done):
                for n in picks:
                    e = SUMMED + n
                    if n == 0:
                        dve.wait_ge(outs, k * PICKED + 1)
                        dve.tensor_tensor(dst[:, :], pick_bank[0][:, :], mask[:, e, :], ALU.mult).then_inc(done, 1)
                    else:
                        wait_for(outs, k * PICKED + n + 1, 4 + n)
                        wait_for(done, k * PICKED + n, 8 + n)
                        dve.copy_predicated(dst[:, :], mask[:, e, :].bitcast(mybir.dt.uint16), pick_bank[n % 3][:, :]
                                            ).then_inc(done, 1)

            def add_summed(k, dst, psum, picked, done):
                dve.wait_ge(picked, (k + 1) * PICKED)
                dve.wait_ge(psum, k + 1)
                dve.tensor_tensor(dst[:, :], dst[:, :], sum_bank[:, :], ALU.add).then_inc(done, 1)

            def choose(k):
                dve.wait_ge(logits_psum, k + 1)
                dve.tensor_tensor(logits[:, :, :], logits_bank[:, 0:NT * E].rearrange("p (t e) -> p t e", e=E),
                                  bg_sb[:, :].unsqueeze(1).broadcast_to([P, NT, E]), ALU.add).then_inc(argmax_step, 1)
                dve.wait_ge(argmax_step, 5 * k + 1)
                dve.tensor_reduce(best[:, :], logits[:, :, :], AX.X, ALU.max).then_inc(argmax_step, 1)
                dve.wait_ge(argmax_step, 5 * k + 2)
                dve.tensor_tensor(ranked[:, :, :], logits[:, :, :], best[:, :].unsqueeze(2).broadcast_to([P, NT, E]),
                                  ALU.is_equal).then_inc(argmax_step, 1)
                dve.wait_ge(argmax_step, 5 * k + 3)
                dve.tensor_tensor(ranked[:, :, :], ranked[:, :, :], rank[:, :].unsqueeze(1).broadcast_to([P, NT, E]),
                                  ALU.mult).then_inc(argmax_step, 1)
                dve.wait_ge(argmax_step, 5 * k + 4)
                dve.tensor_reduce(best[:, :], ranked[:, :, :], AX.X, ALU.max).then_inc(argmax_step, 1)
                dve.wait_ge(argmax_step, 5 * k + 5)
                dve.tensor_tensor(chosen[:, :, :], ranked[:, :, :], best[:, :].unsqueeze(2).broadcast_to([P, NT, E]),
                                  ALU.is_equal).then_inc(chosen_ready, 1)

            def slots(g, parity):
                def pick_h(picks):
                    if live(g):
                        if picks[0] == 0:
                            dve.wait_ge(spread_ready, (g + 1) * E)
                            if not first(g):
                                dve.wait_ge(h_ready, g)
                        pick_outs(g, picks, h_pick, spread[:, parity, :, :], h_outs, h_picked)

                def pick_y(picks):
                    if live(g - 1):
                        if picks[0] == 0 and not first(g - 1):
                            dve.wait_ge(back_psum, g - 1)
                        pick_outs(g - 1, picks, yT_sb, spread[:, 1 - parity, :, :], y_outs, y_picked)

                pick_h((0,))
                pick_h((1,))
                if live(g + 1):
                    choose(g + 1)
                pick_h((2,))
                pick_h((3,))
                if isinstance(g, int) and g == -1:
                    first_stats(B - 1)
                if live(g + 1):
                    wait_for(chosenT_psum, g + 2, 4)
                    dve.tensor_copy(chosenT[:, bass.ds(g + 1, 1), :].rearrange("e n s -> e (n s)"),
                                    chosenT_bank[0:E, :]).then_inc(chosenT_ready, 1)
                if live(g - 2):
                    if not first(g - 2):
                        dve.wait_ge(out_ready, g - 2)
                    dve.wait_ge(x1_kept, 16 * (g - 1))
                    dve.wait_ge(back_psum, g - 1)
                    dve.tensor_tensor(r2[:, :, :], back_bank[:, :].rearrange("p (t c) -> p t c", c=C),
                                      x_sb[:, bass.ds((g - 2) * NT, NT), :], ALU.add).then_inc(r2_ready, 1)
                pick_h((4,))
                if live(g):
                    add_summed(g, h_pick, h_psum, h_picked, h_summed)
                if live(g - 2):
                    wait_for(r2_ready, g - 1, 2)
                    for i in range(NT):
                        dve.bn_stats(stats[:, i, :], r2[:, i, :]).then_inc(r2_stats, 1)
                if live(g - 2):
                    wait_for(r2_stats, (g - 1) * NT, 3)
                    for i in range(NT):
                        last = dve.bn_aggr(aggr[:, i, :], stats[:, i, :])
                    last.then_inc(r2_aggr, 1)
                pick_y((0,))
                pick_y((1,))
                if live(g + 2):
                    if not first(g + 2):
                        dve.wait_ge(x1T_psum, g + 2)
                        dve.wait_ge(x1_kept, 16 * (g + 2))
                    if isinstance(g, int) and g + 2 == B - 1:
                        dve.wait_ge(rstd1_ready, 2)
                    for i in range(NT):
                        tile = (g + 2) * NT + i
                        last = dve.tensor_scalar(x1_now[:, i, :],
                                                 x_sb[:, bass.ds(tile, 1), :].rearrange("p n c -> p (n c)"),
                                                 meanvar[:, bass.ds(tile, 1), 0], rstd1[:, bass.ds(tile, 1)],
                                                 ALU.subtract, ALU.mult)
                    last.then_inc(x1_ready, 1)
                if live(g):
                    dve.wait_ge(h_rounded, g + 1)
                    dve.tensor_tensor(h_lo[:, parity, :], h_32[:, :], h_hi[:, parity, :].bitcast(F32), ALU.subtract
                                      ).then_inc(h_split, 1)
                pick_y((2,))
                pick_y((3,))
                if live(g + 2):
                    dve.wait_ge(x1T_rounded, g + 3)
                    dve.tensor_tensor(x1T_lo[:, parity, :], x1T_bank[:, :], x1T_hi[:, parity, :].bitcast(F32),
                                      ALU.subtract).then_inc(x1T_split, 1)
                pick_y((4,))
                if live(g - 1):
                    add_summed(g - 1, yT_sb, yT_psum, y_picked, yT_summed)

            dve.wait_ge(bg_loaded, 16)
            dve.wait_ge(rstd1_ready, 1)
            expert_slots(dve, slots)


def kernel(**inputs):
    import numpy as _np
    import concourse.bacc as _bacc
    from concourse import mybir as _mybir
    from concourse.bass_utils import run_bass_kernel_spmd as _run

    a = {k[3:]: _np.asarray(v) for k, v in inputs.items()}
    x = a["attn_x"]
    B, S, C = x.shape
    H, D, _ = a["attn_w_q"].shape
    E = a["ffn_W1"].shape[0]
    pairs = H * D // 128
    arrays = {
        "x": x.reshape(B * S, C),
        "xT": x.transpose(0, 2, 1),
        "wq": a["attn_w_q"].reshape(pairs, 128, C),
        "wk": a["attn_w_k"].reshape(pairs, 128, C),
        "wv": a["attn_w_v"].reshape(pairs, 128, C),
        "wo": a["attn_w_o"].reshape(pairs, 128, C),
        "Wg": a["ffn_Wg"],
        "bg": a["ffn_bg"].reshape(1, E),
        "W1": a["ffn_W1"].transpose(1, 0, 2),
        "W2": a["ffn_W2"].transpose(1, 0, 2),
        "b12": _np.concatenate([a["ffn_b1"], a["ffn_b2"]], axis=1),
    }
    arrays = {f"in_{k}": _np.ascontiguousarray(v) for k, v in arrays.items()}
    nc = _bacc.Bacc("TRN2", target_bir_lowering=False, num_devices=1)
    args = [nc.dram_tensor(k, v.shape, _mybir.dt.from_np(v.dtype), kind="ExternalInput").ap() for k, v in arrays.items()]
    out = nc.dram_tensor("out", (B * S, C), _mybir.dt.float32, kind="ExternalOutput").ap()
    layer(nc, *args, out)
    r = _run(nc, [arrays], core_ids=[0])
    return r.results[0]["out"].reshape(B, S, C)
```
